# Optimizing a Trainium2 kernel written in Bass

```python
import numpy as np
import jax
import jax.numpy as jnp

def _softmax(x, axis=-1):
    return jax.nn.softmax(x, axis=axis)

def _gelu(x):
    return jax.nn.gelu(x, approximate=True)

def _silu(x):
    return jax.nn.silu(x)

def _sigmoid(x):
    return jax.nn.sigmoid(x)

def _layernorm(x, axis=-1, eps=1e-05):
    m = jnp.mean(x, axis=axis, keepdims=True)
    v = jnp.var(x, axis=axis, keepdims=True)
    return (x - m) / jnp.sqrt(v + eps)

def _scatter_add(tgt, idx, src, axis=0):
    return tgt.at[idx].add(src)

def _segment_sum(src, seg, n):
    return jax.ops.segment_sum(src, seg, n)
kernel_name = 'mk_macaron_d1_jaxref_r4_90f700'

def setup_inputs(seed: int=0):
    np.random.seed(seed)
    _w = jnp.asarray

    def _L0_attn_setup():
        import jax, jax.numpy as jnp
        import numpy as np
        D = 256
        H = 16
        KVH = 4
        HD = D // H
        LAT = 64
        WIN = 64
        B, S = (1, 512)
        BASE_G, BASE_L = (1000000.0, 10000.0)
        EPS = 1e-06

        def rmsnorm(x, w):
            return x * jax.lax.rsqrt(jnp.mean(x * x, axis=-1, keepdims=True) + EPS) * w

        def qk_norm(x):
            return x * jax.lax.rsqrt(jnp.mean(x * x, axis=-1, keepdims=True) + EPS)

        def rope(x, base):
            s, hd = (x.shape[-2], x.shape[-1])
            inv_freq = 1.0 / base ** (jnp.arange(0, hd, 2, dtype=jnp.float32) / hd)
            freqs = jnp.arange(s, dtype=jnp.float32)[:, None] * inv_freq[None, :]
            cos, sin = (jnp.cos(freqs), jnp.sin(freqs))
            xe, xo = (x[..., ::2], x[..., 1::2])
            out = jnp.stack([xe * cos - xo * sin, xe * sin + xo * cos], axis=-1)
            return out.reshape(x.shape)

        def split_heads(x, n_heads):
            b, s, _ = x.shape
            return x.reshape(b, s, n_heads, HD).transpose(0, 2, 1, 3)

        def repeat_kv(x):
            return jnp.repeat(x, H // KVH, axis=1)

        def sdpa(q, k, v, mask):
            scores = jnp.einsum('bhqd,bhkd->bhqk', q, k) / np.sqrt(HD).astype(np.float32)
            scores = jnp.where(mask, scores, jnp.float32(-1e+30))
            probs = jax.nn.softmax(scores, axis=-1)
            return jnp.einsum('bhqk,bhkd->bhqd', probs, v)

        def merge_heads(x):
            b, h, s, hd = x.shape
            return x.transpose(0, 2, 1, 3).reshape(b, s, h * hd)

        def global_latent_attn(x, wq, w_kv_down, w_k_up, w_v_up, wo):
            q = split_heads(x @ wq, H)
            latent = x @ w_kv_down
            k = split_heads(latent @ w_k_up, KVH)
            v = split_heads(latent @ w_v_up, KVH)
            q, k = (rope(q, BASE_G), rope(k, BASE_G))
            q, k = (qk_norm(q), qk_norm(k))
            k, v = (repeat_kv(k), repeat_kv(v))
            i = jnp.arange(x.shape[1])
            causal = i[:, None] >= i[None, :]
            return merge_heads(sdpa(q, k, v, causal)) @ wo

        def local_gqa_attn(x, wq, wk, wv, wo):
            q = split_heads(x @ wq, H)
            k = split_heads(x @ wk, KVH)
            v = split_heads(x @ wv, KVH)
            q, k = (rope(q, BASE_L), rope(k, BASE_L))
            q, k = (qk_norm(q), qk_norm(k))
            k, v = (repeat_kv(k), repeat_kv(v))
            i = jnp.arange(x.shape[1])
            diff = i[:, None] - i[None, :]
            mask = (diff >= 0) & (diff < WIN)
            return merge_heads(sdpa(q, k, v, mask)) @ wo
        key = jax.random.key(seed)
        ks = jax.random.split(key, 12)
        std = 0.02
        return {'hidden': jax.random.normal(ks[0], (B, S, D), dtype=jnp.float32), 'norm1_w': jnp.ones((D,), jnp.float32), 'norm2_w': jnp.ones((D,), jnp.float32), 'g_wq': jax.random.normal(ks[1], (D, H * HD), jnp.float32) * std, 'g_kv_down': jax.random.normal(ks[2], (D, LAT), jnp.float32) * std, 'g_k_up': jax.random.normal(ks[3], (LAT, KVH * HD), jnp.float32) * std, 'g_v_up': jax.random.normal(ks[4], (LAT, KVH * HD), jnp.float32) * std, 'g_wo': jax.random.normal(ks[5], (D, D), jnp.float32) * std, 'l_wq': jax.random.normal(ks[6], (D, H * HD), jnp.float32) * std, 'l_wk': jax.random.normal(ks[7], (D, KVH * HD), jnp.float32) * std, 'l_wv': jax.random.normal(ks[8], (D, KVH * HD), jnp.float32) * std, 'l_wo': jax.random.normal(ks[9], (D, D), jnp.float32) * std}
    _L0_attn_in = _L0_attn_setup()

    def _L0_ffn_setup():
        import jax, jax.numpy as jnp
        import numpy as np
        B, T, C, D = (2, 1024, 256, 128)
        E = 8
        MIN_E = 2
        EPS = 1e-12
        NEG = -1000000000.0

        def _xavier(key, shape, fan_in, fan_out):
            bound = (6.0 / (fan_in + fan_out)) ** 0.5
            return jax.random.uniform(key, shape, jnp.float32, -bound, bound)

        def _forward(hidden_states, sim_matrix, gates, q_proj, k_proj, v_proj, o_proj):
            b, t, c = hidden_states.shape
            x = hidden_states.reshape(b * t, c)
            xn = x / jnp.maximum(jnp.linalg.norm(x, axis=-1, keepdims=True), EPS)
            sn = sim_matrix / jnp.maximum(jnp.linalg.norm(sim_matrix, axis=0, keepdims=True), EPS)
            logits = xn @ sn - jax.nn.sigmoid(gates)
            gated = jax.nn.relu(logits)
            mask = (gated > 0).astype(logits.dtype)
            inactive = jnp.sum(mask, axis=1) == 0
            top_idx = jax.lax.top_k(logits, MIN_E)[1]
            n = mask.shape[0]
            fb = jnp.zeros_like(mask).at[jnp.arange(n)[:, None], top_idx].set(1.0)
            mask = jnp.where(inactive[:, None] & (fb > 0), 1.0, mask)
            masked_logits = jnp.where(mask > 0, gated, NEG)
            routing_weights = jax.nn.softmax(masked_logits, axis=-1)
            m = jax.lax.stop_gradient(mask)
            q = jnp.einsum('tc,ecd,te->td', x, q_proj, m)
            k = jnp.einsum('tc,ecd,te->td', x, k_proj, m)
            v = jnp.einsum('tc,ecd,te->td', x, v_proj, m)
            qh = q.reshape(b, t, D)
            kh = k.reshape(b, t, D)
            vh = v.reshape(b, t, D)
            scores = jnp.einsum('bqd,bkd->bqk', qh, kh) / jnp.sqrt(jnp.asarray(D, qh.dtype))
            causal = jnp.tril(jnp.ones((t, t), bool))
            scores = jnp.where(causal, scores, jnp.finfo(scores.dtype).min)
            attn = jax.nn.softmax(scores, axis=-1)
            attn_out = jnp.einsum('bqk,bkd->bqd', attn, vh).reshape(b * t, D)
            final = jnp.einsum('td,edc,te->tc', attn_out, o_proj, m * routing_weights)
            return final.reshape(b, t, c)
        key = jax.random.key(seed)
        k = jax.random.split(key, 6)
        hidden_states = jax.random.normal(k[0], (B, T, C), jnp.float32)
        sim_matrix = jax.random.normal(k[1], (C, E), jnp.float32)
        gates = jnp.zeros((E,), jnp.float32)
        q_proj = _xavier(k[2], (E, C, D), C, D)
        k_proj = _xavier(k[3], (E, C, D), C, D)
        v_proj = _xavier(k[4], (E, C, D), C, D)
        o_proj = _xavier(k[5], (E, D, C), D, C)
        return dict(hidden_states=hidden_states, sim_matrix=sim_matrix, gates=gates, q_proj=q_proj, k_proj=k_proj, v_proj=v_proj, o_proj=o_proj)
    _L0_ffn_in = _L0_ffn_setup()
    _d = {'L0_attn_hidden': _L0_attn_in['hidden'], 'L0_attn_norm1_w': _L0_attn_in['norm1_w'], 'L0_attn_norm2_w': _L0_attn_in['norm2_w'], 'L0_attn_g_wq': _L0_attn_in['g_wq'], 'L0_attn_g_kv_down': _L0_attn_in['g_kv_down'], 'L0_attn_g_k_up': _L0_attn_in['g_k_up'], 'L0_attn_g_v_up': _L0_attn_in['g_v_up'], 'L0_attn_g_wo': _L0_attn_in['g_wo'], 'L0_attn_l_wq': _L0_attn_in['l_wq'], 'L0_attn_l_wk': _L0_attn_in['l_wk'], 'L0_attn_l_wv': _L0_attn_in['l_wv'], 'L0_attn_l_wo': _L0_attn_in['l_wo'], 'L0_ffn_sim_matrix': _L0_ffn_in['sim_matrix'], 'L0_ffn_gates': _L0_ffn_in['gates'], 'L0_ffn_q_proj': _L0_ffn_in['q_proj'], 'L0_ffn_k_proj': _L0_ffn_in['k_proj'], 'L0_ffn_v_proj': _L0_ffn_in['v_proj'], 'L0_ffn_o_proj': _L0_ffn_in['o_proj']}
    _x0 = _d['L0_attn_hidden']
    _d['L0_attn_hidden'] = jax.random.normal(jax.random.fold_in(jax.random.key(seed), 1), (4, 1024, 256), dtype=_x0.dtype)
    del _x0
    return _d

def reference(L0_attn_hidden, L0_attn_norm1_w, L0_attn_norm2_w, L0_attn_g_wq, L0_attn_g_kv_down, L0_attn_g_k_up, L0_attn_g_v_up, L0_attn_g_wo, L0_attn_l_wq, L0_attn_l_wk, L0_attn_l_wv, L0_attn_l_wo, L0_ffn_sim_matrix, L0_ffn_gates, L0_ffn_q_proj, L0_ffn_k_proj, L0_ffn_v_proj, L0_ffn_o_proj):

    def _L0_attn_ref(hidden, norm1_w, norm2_w, g_wq, g_kv_down, g_k_up, g_v_up, g_wo, l_wq, l_wk, l_wv, l_wo):
        import jax, jax.numpy as jnp
        import numpy as np
        D = 256
        H = 16
        KVH = 4
        HD = D // H
        LAT = 64
        WIN = 64
        B, S = (1, 512)
        BASE_G, BASE_L = (1000000.0, 10000.0)
        EPS = 1e-06

        def rmsnorm(x, w):
            return x * jax.lax.rsqrt(jnp.mean(x * x, axis=-1, keepdims=True) + EPS) * w

        def qk_norm(x):
            return x * jax.lax.rsqrt(jnp.mean(x * x, axis=-1, keepdims=True) + EPS)

        def rope(x, base):
            s, hd = (x.shape[-2], x.shape[-1])
            inv_freq = 1.0 / base ** (jnp.arange(0, hd, 2, dtype=jnp.float32) / hd)
            freqs = jnp.arange(s, dtype=jnp.float32)[:, None] * inv_freq[None, :]
            cos, sin = (jnp.cos(freqs), jnp.sin(freqs))
            xe, xo = (x[..., ::2], x[..., 1::2])
            out = jnp.stack([xe * cos - xo * sin, xe * sin + xo * cos], axis=-1)
            return out.reshape(x.shape)

        def split_heads(x, n_heads):
            b, s, _ = x.shape
            return x.reshape(b, s, n_heads, HD).transpose(0, 2, 1, 3)

        def repeat_kv(x):
            return jnp.repeat(x, H // KVH, axis=1)

        def sdpa(q, k, v, mask):
            scores = jnp.einsum('bhqd,bhkd->bhqk', q, k) / np.sqrt(HD).astype(np.float32)
            scores = jnp.where(mask, scores, jnp.float32(-1e+30))
            probs = jax.nn.softmax(scores, axis=-1)
            return jnp.einsum('bhqk,bhkd->bhqd', probs, v)

        def merge_heads(x):
            b, h, s, hd = x.shape
            return x.transpose(0, 2, 1, 3).reshape(b, s, h * hd)

        def global_latent_attn(x, wq, w_kv_down, w_k_up, w_v_up, wo):
            q = split_heads(x @ wq, H)
            latent = x @ w_kv_down
            k = split_heads(latent @ w_k_up, KVH)
            v = split_heads(latent @ w_v_up, KVH)
            q, k = (rope(q, BASE_G), rope(k, BASE_G))
            q, k = (qk_norm(q), qk_norm(k))
            k, v = (repeat_kv(k), repeat_kv(v))
            i = jnp.arange(x.shape[1])
            causal = i[:, None] >= i[None, :]
            return merge_heads(sdpa(q, k, v, causal)) @ wo

        def local_gqa_attn(x, wq, wk, wv, wo):
            q = split_heads(x @ wq, H)
            k = split_heads(x @ wk, KVH)
            v = split_heads(x @ wv, KVH)
            q, k = (rope(q, BASE_L), rope(k, BASE_L))
            q, k = (qk_norm(q), qk_norm(k))
            k, v = (repeat_kv(k), repeat_kv(v))
            i = jnp.arange(x.shape[1])
            diff = i[:, None] - i[None, :]
            mask = (diff >= 0) & (diff < WIN)
            return merge_heads(sdpa(q, k, v, mask)) @ wo
        x = hidden
        x = x + global_latent_attn(rmsnorm(x, norm1_w), g_wq, g_kv_down, g_k_up, g_v_up, g_wo)
        x = x + local_gqa_attn(rmsnorm(x, norm2_w), l_wq, l_wk, l_wv, l_wo)
        return x

    def _L0_ffn_ref(hidden_states, sim_matrix, gates, q_proj, k_proj, v_proj, o_proj):
        import jax, jax.numpy as jnp
        import numpy as np
        B, T, C, D = (2, 1024, 256, 128)
        E = 8
        MIN_E = 2
        EPS = 1e-12
        NEG = -1000000000.0

        def _xavier(key, shape, fan_in, fan_out):
            bound = (6.0 / (fan_in + fan_out)) ** 0.5
            return jax.random.uniform(key, shape, jnp.float32, -bound, bound)

        def _forward(hidden_states, sim_matrix, gates, q_proj, k_proj, v_proj, o_proj):
            b, t, c = hidden_states.shape
            x = hidden_states.reshape(b * t, c)
            xn = x / jnp.maximum(jnp.linalg.norm(x, axis=-1, keepdims=True), EPS)
            sn = sim_matrix / jnp.maximum(jnp.linalg.norm(sim_matrix, axis=0, keepdims=True), EPS)
            logits = xn @ sn - jax.nn.sigmoid(gates)
            gated = jax.nn.relu(logits)
            mask = (gated > 0).astype(logits.dtype)
            inactive = jnp.sum(mask, axis=1) == 0
            top_idx = jax.lax.top_k(logits, MIN_E)[1]
            n = mask.shape[0]
            fb = jnp.zeros_like(mask).at[jnp.arange(n)[:, None], top_idx].set(1.0)
            mask = jnp.where(inactive[:, None] & (fb > 0), 1.0, mask)
            masked_logits = jnp.where(mask > 0, gated, NEG)
            routing_weights = jax.nn.softmax(masked_logits, axis=-1)
            m = jax.lax.stop_gradient(mask)
            q = jnp.einsum('tc,ecd,te->td', x, q_proj, m)
            k = jnp.einsum('tc,ecd,te->td', x, k_proj, m)
            v = jnp.einsum('tc,ecd,te->td', x, v_proj, m)
            qh = q.reshape(b, t, D)
            kh = k.reshape(b, t, D)
            vh = v.reshape(b, t, D)
            scores = jnp.einsum('bqd,bkd->bqk', qh, kh) / jnp.sqrt(jnp.asarray(D, qh.dtype))
            causal = jnp.tril(jnp.ones((t, t), bool))
            scores = jnp.where(causal, scores, jnp.finfo(scores.dtype).min)
            attn = jax.nn.softmax(scores, axis=-1)
            attn_out = jnp.einsum('bqk,bkd->bqd', attn, vh).reshape(b * t, D)
            final = jnp.einsum('td,edc,te->tc', attn_out, o_proj, m * routing_weights)
            return final.reshape(b, t, c)
        return _forward(hidden_states, sim_matrix, gates, q_proj, k_proj, v_proj, o_proj)
    x = L0_attn_hidden
    x = x + 0.5 * _L0_ffn_ref(_layernorm(x, axis=-1), L0_ffn_sim_matrix, L0_ffn_gates, L0_ffn_q_proj, L0_ffn_k_proj, L0_ffn_v_proj, L0_ffn_o_proj)
    x = x + _L0_attn_ref(_layernorm(x, axis=-1), L0_attn_norm1_w, L0_attn_norm2_w, L0_attn_g_wq, L0_attn_g_kv_down, L0_attn_g_k_up, L0_attn_g_v_up, L0_attn_g_wo, L0_attn_l_wq, L0_attn_l_wk, L0_attn_l_wv, L0_attn_l_wo)
    x = x + 0.5 * _L0_ffn_ref(_layernorm(x, axis=-1), L0_ffn_sim_matrix, L0_ffn_gates, L0_ffn_q_proj, L0_ffn_k_proj, L0_ffn_v_proj, L0_ffn_o_proj)
    return x

_drawn_inputs = setup_inputs


def setup_inputs(seed=0):
    import zlib

    import numpy as np

    out = dict(_drawn_inputs(seed))
    spreads = {'L0_attn_norm1_w': (1.0, 0.6), 'L0_attn_norm2_w': (1.0, 0.6), 'L0_ffn_gates': (0.0, 0.1)}
    factors = {'L0_attn_g_wq': 7.488,
     'L0_attn_g_kv_down': 8.0,
     'L0_attn_g_k_up': 8.0,
     'L0_attn_g_v_up': 6.025,
     'L0_attn_g_wo': 5.862,
     'L0_attn_l_wq': 3.366,
     'L0_attn_l_wk': 3.157}
    for name, (base, spread) in spreads.items():
        noise = np.random.default_rng([zlib.crc32(name.encode()), seed]).standard_normal(out[name].shape)
        drawn = base * np.exp(spread * noise) if base else spread * noise
        out[name] = jnp.asarray(drawn.astype(out[name].dtype))
    for name, factor in factors.items():
        out[name] = (out[name] * factor).astype(out[name].dtype)
    return out
```

```python
import concourse.bass as bass
from concourse import mybir
from contextlib import ExitStack

P = 128
B, S, C = 4, 1024, 256
TILES = S // P
CT = C // P
HALF = 512
E, D = 8, 128
H, KVH, HD = 16, 4, 16
LAT = 64
WIN = 64
QK = (H + KVH) * HD
QKV = QK + KVH * HD
GW = LAT + H * HD
LW = QKV
AW = GW + LW + 2 * C
SPAN = P + WIN
XM = 4
PR = 4

K_ID, K_NEG, K_WIN, K_TRI8, K_COS = 0, 128, 256, 256 + SPAN, 256 + SPAN + 64
K_TRI = K_COS + 4 * 64
K_ALL = K_TRI + 128

F32, F16, F32R = mybir.dt.float32, mybir.dt.float16, mybir.dt.float32r
ALU, ACT, AX = mybir.AluOpType, mybir.ActivationFunctionType, mybir.AxisListType


class Mem:

    def __init__(self, nc, ctx):
        def sb(name, shape, dt=F32):
            return ctx.enter_context(nc.sbuf_tensor(name, shape, dt))
        self.const = sb("const", [P, K_ALL])
        self.ident16 = sb("ident16", [P, P], F16)
        self.zeros16 = sb("zeros16", [P, HALF], F16)
        self.half = sb("half", [P, 4 * (H + KVH)])
        self.w_hi = sb("w_hi", [P, 3, E * CT, D], F32R)
        self.w_lo = sb("w_lo", [P, 3, E * CT, D], F32R)
        self.o_hi = sb("o_hi", [P, E * C], F32R)
        self.o_lo = sb("o_lo", [P, E * C], F32R)
        self.a_hi = sb("a_hi", [P, CT, AW], F32R)
        self.a_lo = sb("a_lo", [P, CT, AW], F32R)
        self.kv_up = sb("kv_up", [LAT, 2 * KVH * HD])
        self.sn_hi = sb("sn_hi", [P, CT, E], F32R)
        self.sn_lo = sb("sn_lo", [P, CT, E], F32R)
        self.sig = sb("sig", [P, E])
        self.norm_w = sb("norm_w", [P, 2, CT])
        self.xa = sb("xa", [P, TILES, C])
        self.xb = sb("xb", [P, TILES, C])
        self.xn = sb("xn", [P, TILES, C])
        self.xt_hi = sb("xt_hi", [P, CT, S], F32R)
        self.xt_lo = sb("xt_lo", [P, CT, S], F32R)
        self.stats = sb("stats", [P, TILES, 6])
        self.mv = sb("mv", [P, TILES, 2])
        self.small = sb("small", [P, 8, TILES])
        self.arena_bytes = 78 * 1024
        self.nc, self.base, self.views = nc, nc.sbuf_base, 0
        sb("arena", [P, self.arena_bytes // 4])
        self.ps = ctx.enter_context(nc.psum_tensor("ps", [P, 8, HALF], F32))

    def at(self, name, word, n, dt=F32):
        words = n // 2 if dt == F16 else n
        assert (word + words) * 4 <= self.arena_bytes, (name, word + words)
        self.views += 1
        return self.nc.alloc_sbuf_tensor_at(f"{name}_{self.views}", [P, n], dt, offset=self.base + 4 * word, align_bytes=4)[:]

    def carve(self, *parts):
        word, views = 0, {}
        for name, n, dt in parts:
            views[name] = self.at(name, word, n, dt)
            word += n // 2 if dt == F16 else n
        return views


class Chain:

    def __init__(self, eng, sem):
        self.eng, self.sem, self.n = eng, sem, 0

    def done(self, ins):
        self.n += 1
        ins.then_inc(self.sem, 1)

    def wait(self):
        self.eng.wait_ge(self.sem, self.n)

    def link(self, ins):
        self.done(ins)
        self.wait()


def semaphores(nc, ctx, stage, names):
    return {name: ctx.enter_context(nc.semaphore(f"{stage}_{name}")) for name in names.split()}


def rsqrt_pool(nc, m, pool, chain, out, x, scale, eps, n):
    chain.link(nc.gpsimd.tensor_scalar(out, x, scale, eps, ALU.mult, ALU.add))
    return nc.gpsimd.tensor_tensor(out, out, n, ALU.pow)


SETUP_SEMS = "const w oo aw misc gates cast stage hi split chain pchain pre sq ss rn sig exp"


def setup(nc, m, q, ins):
    v = m.carve(("wst", 3 * E * CT * D, F32), ("ost", E * C, F32), ("ast", CT * AW, F32),
                ("sim", CT * E, F32), ("sq", CT * E, F32), ("ones", P, F32), ("gt", E, F32), ("rn", E, F32))
    wst = v["wst"].rearrange("p (w k d) -> p w k d", w=3, d=D)
    ast = v["ast"].rearrange("p (t n) -> p t n", t=CT)
    sim = v["sim"].rearrange("p (t e) -> p t e", t=CT)
    sq = v["sq"].rearrange("p (t e) -> p t e", t=CT)
    ones, gt, rn = v["ones"], v["gt"], v["rn"]
    norm_ps = m.ps[:, 0, 0:E]

    with nc.Block() as block:
        @block.sync
        def _(sp):
            sp.dma_start(m.const[:], ins["const"]).then_inc(q["const"], 16)
            sp.dma_start(sim, ins["L0_ffn_sim_matrix"].rearrange("(t p) e -> p t e", p=P)).then_inc(q["misc"], 16)
            sp.dma_start(m.norm_w[:, 0, :], ins["L0_attn_norm1_w"].rearrange("(t p) -> p t", p=P),
                         allow_slow_non_contiguous=True).then_inc(q["misc"], 16)
            sp.dma_start(m.norm_w[:, 1, :], ins["L0_attn_norm2_w"].rearrange("(t p) -> p t", p=P),
                         allow_slow_non_contiguous=True).then_inc(q["misc"], 16)
            sp.dma_start(gt, ins["L0_ffn_gates"].partition_broadcast(P)).then_inc(q["misc"], 16)
            for i, n in enumerate(("q", "k", "v")):
                sp.dma_start(wst[:, i], ins[f"L0_ffn_{n}_proj"].rearrange("e (t p) d -> p (e t) d", p=P)).then_inc(q["w"], 16)
            sp.dma_start(v["ost"].rearrange("p (e c) -> p e c", e=E),
                         ins["L0_ffn_o_proj"].rearrange("e d c -> d e c")).then_inc(q["oo"], 16)

        @block.gpsimd
        def _(pool):
            chain = Chain(pool, q["pchain"])
            chain.done(nc.gpsimd.memset(m.half[:], -0.5))
            chain.done(nc.gpsimd.memset(m.zeros16[:], 0.0))
            nc.gpsimd.memset(ones, 1.0).then_inc(q["pre"], 1)
            pool.wait_ge(q["ss"], 1)
            chain.wait()
            nc.gpsimd.tensor_tensor(rn, rn, m.half[:, 0:E], ALU.pow).then_inc(q["rn"], 1)

        @block.tensor
        def _(pe):
            pe.wait_ge(q["pre"], 1)
            pe.wait_ge(q["sq"], 1)
            for t in range(CT):
                ins_ = nc.tensor.matmul(norm_ps, ones, sq[:, t], start=t == 0, stop=t == CT - 1)
            ins_.then_inc(q["stage"], 1)

        @block.scalar
        def _(act):
            at = 0
            for name, n in (("L0_attn_g_kv_down", LAT), ("L0_attn_g_wq", C), ("L0_attn_l_wq", C), ("L0_attn_l_wk", KVH * HD),
                            ("L0_attn_l_wv", KVH * HD), ("L0_attn_g_wo", C), ("L0_attn_l_wo", C)):
                act.dma_start(ast[:, :, at:at + n], ins[name].rearrange("(t p) n -> p t n", p=P)).then_inc(q["aw"], 16)
                at += n
            act.dma_start(m.kv_up[:, 0:KVH * HD], ins["L0_attn_g_k_up"]).then_inc(q["aw"], 16)
            act.dma_start(m.kv_up[:, KVH * HD:], ins["L0_attn_g_v_up"]).then_inc(q["aw"], 16)
            act.wait_ge(q["misc"], 64)
            nc.scalar.activation(gt, gt, ACT.Exp, scale=-1.0).then_inc(q["exp"], 1)
            act.wait_ge(q["w"], 48)
            nc.scalar.copy(m.w_hi[:], wst).then_inc(q["hi"], 1)
            act.wait_ge(q["oo"], 16)
            nc.scalar.copy(m.o_hi[:], v["ost"]).then_inc(q["hi"], 1)
            act.wait_ge(q["cast"], 4)
            nc.scalar.copy(m.a_hi[:], ast).then_inc(q["hi"], 1)

        @block.vector
        def _(dve):
            chain = Chain(dve, q["chain"])
            dve.wait_ge(q["misc"], 64)
            nc.vector.tensor_tensor(sq, sim, sim, ALU.mult).then_inc(q["sq"], 1)
            dve.wait_ge(q["const"], 16)
            nc.vector.tensor_copy(m.ident16[:], m.const[:, K_ID:K_ID + P])
            dve.wait_ge(q["exp"], 1)
            chain.link(nc.vector.tensor_scalar(gt, gt, 1.0, None, ALU.add))
            chain.done(nc.vector.reciprocal(m.sig[:], gt))
            dve.wait_ge(q["stage"], 1)
            nc.vector.tensor_scalar(rn, norm_ps, 1e-24, None, ALU.max).then_inc(q["ss"], 1)
            dve.wait_ge(q["aw"], 16 * 9)
            for t in range(CT):
                for i, (a, n) in enumerate(((0, GW), (GW, LW))):
                    nc.vector.tensor_scalar(ast[:, t, a:a + n], ast[:, t, a:a + n], m.norm_w[:, i, t:t + 1], None,
                                            ALU.mult).then_inc(q["cast"], 1)
            dve.wait_ge(q["rn"], 1)
            chain.link(nc.vector.tensor_tensor(sim, sim, rn.unsqueeze(1).to_broadcast([P, CT, E]), ALU.mult))
            chain.link(nc.vector.tensor_copy(m.sn_hi[:], sim))
            chain.done(nc.vector.tensor_tensor(m.sn_lo[:], sim, m.sn_hi[:].bitcast(F32), ALU.subtract))
            dve.wait_ge(q["hi"], 1)
            nc.vector.tensor_tensor(m.w_lo[:], wst, m.w_hi[:].bitcast(F32), ALU.subtract)
            dve.wait_ge(q["hi"], 2)
            nc.vector.tensor_tensor(m.o_lo[:], v["ost"], m.o_hi[:].bitcast(F32), ALU.subtract)
            dve.wait_ge(q["hi"], 3)
            nc.vector.tensor_tensor(m.a_lo[:], ast, m.a_hi[:].bitcast(F32), ALU.subtract)


def clear(nc, q):
    ids = [s.num for s in q.values()]
    assert max(ids) - min(ids) == len(ids) - 1
    nc.gpsimd.sem_clear(range(min(ids), max(ids) + 1))
    nc.all_engine_barrier()


FFN_SEMS = ("x0 x1 chain pchain var rstd xln ss rn tr hi lo lg m gmax gexp mb xm qkv ev vt v s nm exp ptc pte pv ath atl "
            "zz z res out")


def layernorm(nc, m, dve, chain, q, x, waits):
    for h in range(2):
        waits(h)
        for t in range(4 * h, 4 * h + 4):
            chain.done(nc.vector.bn_stats(m.stats[:, t, :], x[:, t, :]))
        chain.wait()
        for t in range(4 * h, 4 * h + 4):
            chain.done(nc.vector.bn_aggr(m.mv[:, t, :], m.stats[:, t, :]))
        chain.wait()
        nc.vector.tensor_copy(m.small[:, 0, 4 * h:4 * h + 4], m.mv[:, 4 * h:4 * h + 4, 1]).then_inc(q["var"], 1)


def transpose_rows(nc, m, pe, src, h, ct, bank):
    for t in range(4):
        ins = nc.tensor.transpose(m.ps[:, bank, t * P:t * P + P], src[:, 4 * h + t, ct * P:ct * P + P],
                                  m.const[:, K_ID:K_ID + P])
    return ins


def three_pass(nc, out, w_hi, w_lo, x_hi, x_lo, first, last):
    nc.tensor.matmul(out, w_hi, x_hi, start=first, stop=False)
    nc.tensor.matmul(out, w_lo, x_hi, start=False, stop=False)
    return nc.tensor.matmul(out, w_hi, x_lo, start=False, stop=last)


def ffn(nc, m, q, b, x_dram, out_dram, first):
    x, out = (m.xa, m.xb) if first else (m.xb, m.xa)
    v = m.carve(("xmh", XM * CT * HALF, F32R), ("xml", XM * CT * HALF, F32R), ("qt", S, F32), ("kt", S, F32),
                ("vt", HALF, F32), ("v", TILES * D, F32), ("p", 2 * S, F32), ("at_hi", S, F32R), ("at_lo", S, F32R),
                ("m16", TILES * E, F16), ("lg", TILES * E, F32), ("gated", TILES * E, F32), ("mask", TILES * E, F32),
                ("w", TILES * E, F32), ("w2", TILES * E, F32), ("cnt", TILES, F32), ("rsum", TILES, F32),
                ("nmax", TILES, F32), ("rinv", TILES, F32), ("junk", C, F32), ("g", TILES * E * E, F32))
    v["eq"] = m.at("eq", 0, TILES * E * E)
    xmh = v["xmh"].rearrange("p (r t n) -> p r t n", r=XM, t=CT)
    xml = v["xml"].rearrange("p (r t n) -> p r t n", r=XM, t=CT)
    pt = m.at("pt", 0, TILES * HALF).rearrange("p (k n) -> p k n", k=TILES)
    vv = v["v"].rearrange("p (t d) -> p t d", t=TILES)
    pp = v["p"].rearrange("p (r n) -> p r n", r=2)
    te = lambda n: v[n].rearrange("p (t e) -> p t e", t=TILES)
    m16, lg, gated, mask, w, w2 = (te(n) for n in ("m16", "lg", "gated", "mask", "w", "w2"))
    qt, kt, vt, at_hi, at_lo, cnt, rsum, nmax, rinv = (v[n] for n in
        ("qt", "kt", "vt", "at_hi", "at_lo", "cnt", "rsum", "nmax", "rinv"))
    ps = m.ps
    var, rstd, ss, rn = (m.small[:, i, :] for i in range(4))
    XB = [0, 1]
    LG = 2
    MB = [2, 3]
    QB = [4, 5, 6]
    SB = [4, 6]
    PB, AB = 0, 1
    ZB = [2, 3]

    def chunks(i):
        return [(k, min(k + 4, i + 1)) for k in range(0, i + 1, 4)]
    before = [sum(len(chunks(j)) for j in range(i)) for i in range(TILES + 1)]
    turns = range(TILES + 5)

    with nc.Block() as block:
        @block.sync
        def _(sp):
            if first:
                for h, s in enumerate((q["x0"], q["x1"])):
                    sp.dma_start(x[:, 4 * h:4 * h + 4, :],
                                 x_dram[bass.ds(b, 1), h * HALF:(h + 1) * HALF, :].rearrange("b (t p) c -> p (b t) c", p=P)).then_inc(s, 16)
            else:
                for h in range(2):
                    sp.wait_ge(q["res"], h + 1)
                    sp.dma_start(out_dram[bass.ds(b, 1), h * HALF:(h + 1) * HALF, :].rearrange("b (t p) c -> p (b t) c", p=P),
                                 out[:, 4 * h:4 * h + 4, :]).then_inc(q["out"], 16)
                sp.wait_ge(q["out"], 32)

        @block.gpsimd
        def _(pool):
            chain = Chain(pool, q["pchain"])
            for h in range(2):
                pool.wait_ge(q["var"], h + 1)
                r = slice(4 * h, 4 * h + 4)
                rsqrt_pool(nc, m, pool, chain, rstd[:, r], var[:, r], 1.0, 1e-5, m.half[:, 0:4]).then_inc(q["rstd"], 1)
            pool.wait_ge(q["ss"], TILES)
            chain.link(nc.gpsimd.tensor_scalar(rn, ss, 1e-24, None, ALU.max))
            nc.gpsimd.tensor_tensor(rn, rn, m.half[:, 0:TILES], ALU.pow).then_inc(q["rn"], 1)

        @block.vector
        def _(dve):
            chain = Chain(dve, q["chain"])
            layernorm(nc, m, dve, chain, q, x, (lambda h: dve.wait_ge((q["x0"], q["x1"])[h], 16)) if first else (lambda h: None))
            for h in range(2):
                dve.wait_ge(q["rstd"], h + 1)
                for t in range(4 * h, 4 * h + 4):
                    nc.vector.tensor_scalar(m.xn[:, t, :], x[:, t, :], m.mv[:, t, 0:1], rstd[:, t:t + 1],
                                            ALU.subtract, ALU.mult).then_inc(q["xln"], 1)
            for n in range(4):
                h, ct = divmod(n, 2)
                r = slice(h * HALF, (h + 1) * HALF)
                dve.wait_ge(q["hi"], n + 1)
                nc.vector.tensor_tensor(m.xt_lo[:, ct, r], ps[:, XB[ct], :], m.xt_hi[:, ct, r].bitcast(F32),
                                        ALU.subtract).then_inc(q["lo"], 1)
            dve.wait_ge(q["rn"], 1)
            dve.wait_ge(q["lg"], 1)
            full = [P, TILES, E]
            cube = [P, TILES, E, E]
            chain.link(nc.vector.tensor_tensor(lg, ps[:, LG, 0:TILES * E].rearrange("p (t e) -> p t e", t=TILES),
                                               rn.unsqueeze(2).to_broadcast(full), ALU.mult))
            chain.link(nc.vector.tensor_tensor(lg, lg, m.sig[:].unsqueeze(1).to_broadcast(full), ALU.subtract))
            chain.done(nc.vector.tensor_scalar(gated, lg, 0.0, None, ALU.max))
            chain.done(nc.vector.tensor_scalar(mask, lg, 0.0, None, ALU.is_gt))
            g = v["g"].rearrange("p (t e j) -> p t e j", t=TILES, e=E)
            eq = v["eq"].rearrange("p (t e j) -> p t e j", t=TILES, e=E)
            le, lj = lg.unsqueeze(3).to_broadcast(cube), lg.unsqueeze(2).to_broadcast(cube)
            chain.done(nc.vector.tensor_tensor(g, lj, le, ALU.is_gt))
            chain.link(nc.vector.tensor_tensor(eq, lj, le, ALU.is_equal))
            lower = m.const[:, K_TRI8:K_TRI8 + 64].rearrange("p (e j) -> p e j", e=E).unsqueeze(1).to_broadcast(cube)
            chain.link(nc.vector.tensor_tensor(eq, eq, lower, ALU.mult))
            chain.link(nc.vector.tensor_tensor(g, g, eq, ALU.add))
            chain.done(nc.vector.tensor_reduce(w2, g, AX.X, ALU.add))
            chain.done(nc.vector.tensor_reduce(cnt, mask, AX.X, ALU.add))
            chain.link(nc.vector.tensor_reduce(nmax, gated, AX.X, ALU.max))
            chain.done(nc.vector.tensor_scalar(w2, w2, 2.0, None, ALU.is_lt))
            chain.done(nc.vector.tensor_tensor(gated, gated, nmax.unsqueeze(2).to_broadcast(full), ALU.subtract))
            chain.link(nc.vector.tensor_scalar(cnt, cnt, 0.0, None, ALU.is_equal))
            chain.link(nc.vector.tensor_tensor(w2, w2, cnt.unsqueeze(2).to_broadcast(full), ALU.mult))
            chain.link(nc.vector.tensor_tensor(mask, mask, w2, ALU.max))
            nc.vector.tensor_copy(m16, mask).then_inc(q["m"], 1)
            dve.wait_ge(q["gexp"], 1)
            chain.link(nc.vector.tensor_tensor(w, w, mask, ALU.mult))
            chain.link(nc.vector.tensor_reduce(cnt, w, AX.X, ALU.add))
            chain.link(nc.vector.reciprocal(cnt, cnt))
            chain.link(nc.vector.tensor_scalar(cnt, cnt, 0.5, None, ALU.mult))
            chain.link(nc.vector.tensor_tensor(w, w, cnt.unsqueeze(2).to_broadcast(full), ALU.mult))
            for n in range(2 * E):
                h, e = divmod(n, E)
                r = slice(h * HALF, (h + 1) * HALF)
                dve.wait_ge(q["mb"], n + 1)
                if n >= XM:
                    dve.wait_ge(q["qkv"], n - XM + 1)
                mb = ps[:, MB[n % 2], :].unsqueeze(1).to_broadcast([P, CT, HALF])
                for o, i in ((xmh, m.xt_hi), (xml, m.xt_lo)):
                    nc.vector.tensor_tensor(o[:, n % XM], i[:, :, r].bitcast(F32), mb, ALU.mult).then_inc(q["xm"], 1)
            for i in turns:
                if i < TILES:
                    dve.wait_ge(q["s"], i + 1)
                    sc = ps[:, SB[i % 2]:SB[i % 2] + 2, :].rearrange("p b n -> p (b n)")
                    dg = sc[:, i * P:(i + 1) * P]
                    chain.link(nc.vector.tensor_tensor(dg, dg, m.const[:, K_NEG:K_NEG + P], ALU.add))
                    nc.vector.tensor_reduce(nmax[:, i:i + 1], sc[:, 0:(i + 1) * P], AX.X, ALU.max, negate=True).then_inc(q["nm"], 1)
                if 0 <= i - 1 < TILES:
                    j = i - 1
                    for c, (k0, k1) in enumerate(chunks(j)):
                        dve.wait_ge(q["ptc"], before[j] + c + 1)
                        if j == 4 and c == 0:
                            dve.wait_ge(q["pv"], 1)
                        nc.vector.tensor_copy(pt[:, k0:k1, (j % 4) * P:(j % 4 + 1) * P],
                                              ps[:, PB, 0:(k1 - k0) * P].rearrange("p (k n) -> p k n", n=P)).then_inc(q["pte"], 1)
                if i in (4, 9):
                    h = 0 if i == 4 else 1
                    dve.wait_ge(q["ath"], h + 1)
                    nc.vector.tensor_tensor(at_lo[:, h * HALF:(h + 1) * HALF], ps[:, AB, :],
                                            at_hi[:, h * HALF:(h + 1) * HALF].bitcast(F32), ALU.subtract).then_inc(q["atl"], 1)
                if i >= 5:
                    j = i - 5
                    dve.wait_ge(q["exp"], j + 1)
                    chain.link(nc.vector.reciprocal(rinv[:, j:j + 1], rsum[:, j:j + 1]))
                    chain.link(nc.vector.tensor_scalar(w2[:, j, :], w[:, j, :], rinv[:, j:j + 1], None, ALU.mult))
                    for e in range(E):
                        if e % 2 == 0:
                            dve.wait_ge(q["zz"], 4 * j + e // 2 + 1)
                        z = ps[:, ZB[(e // 2) % 2], (e % 2) * C:(e % 2 + 1) * C]
                        src = x if e == 0 else out
                        z_done = nc.vector.scalar_tensor_tensor(out[:, j, :], z, w2[:, j, e:e + 1], src[:, j, :], ALU.mult, ALU.add)
                        z_done.then_inc(q["z"], 1)
                        dve.wait_ge(q["z"], E * j + e + 1)
                    if j % 4 == 3:
                        dve.sem_inc(q["res"], 1)

        @block.scalar
        def _(act):
            for t in range(TILES):
                act.wait_ge(q["xln"], t + 1)
                nc.scalar.activation(v["junk"], m.xn[:, t, :], ACT.Square, accum_out=ss[:, t:t + 1]).then_inc(q["ss"], 1)
                act.wait_ge(q["ss"], t + 1)
                if t % 4 == 3:
                    for ct in range(CT):
                        h = t // 4
                        act.wait_ge(q["tr"], 2 * h + ct + 1)
                        nc.scalar.copy(m.xt_hi[:, ct, h * HALF:(h + 1) * HALF], ps[:, XB[ct], :]).then_inc(q["hi"], 1)
            act.wait_ge(q["m"], 1)
            nc.scalar.activation(w, gated, ACT.Exp).then_inc(q["gexp"], 1)
            for h in range(2):
                r = slice(h * HALF, (h + 1) * HALF)
                act.wait_ge(q["qkv"], E * (h + 1))
                if h:
                    act.wait_ge(q["vt"], 1)
                nc.scalar.activation(qt[:, r], ps[:, QB[0], :], ACT.Copy, scale=float(D) ** -0.5).then_inc(q["ev"], 1)
                nc.scalar.copy(kt[:, r], ps[:, QB[1], :]).then_inc(q["ev"], 1)
                nc.scalar.copy(vt, ps[:, QB[2], :]).then_inc(q["ev"], 1)
                act.wait_ge(q["vt"], h + 1)
                nc.scalar.copy(vv[:, 4 * h:4 * h + 4, :], ps[:, XB[h], :].rearrange("p (t d) -> p t d", t=4)).then_inc(q["v"], 1)
            for i in turns:
                if i < TILES:
                    act.wait_ge(q["nm"], i + 1)
                    if i >= 2:
                        act.wait_ge(q["ptc"], before[i - 1])
                    sc = ps[:, SB[i % 2]:SB[i % 2] + 2, :].rearrange("p b n -> p (b n)")
                    nc.scalar.activation(pp[:, i % 2, 0:(i + 1) * P], sc[:, 0:(i + 1) * P], ACT.Exp, bias=nmax[:, i:i + 1],
                                         accum_out=rsum[:, i:i + 1]).then_inc(q["exp"], 1)
                if i in (4, 9):
                    h = 0 if i == 4 else 1
                    act.wait_ge(q["pv"], h + 1)
                    nc.scalar.copy(at_hi[:, h * HALF:(h + 1) * HALF], ps[:, AB, :]).then_inc(q["ath"], 1)

        @block.tensor
        def _(pe):
            for n in range(4):
                h, ct = divmod(n, 2)
                pe.wait_ge(q["xln"], 4 * h + 4)
                if n >= 2:
                    pe.wait_ge(q["lo"], n - 1)
                transpose_rows(nc, m, pe, m.xn, h, ct, XB[ct]).then_inc(q["tr"], 1)
            pe.wait_ge(q["lo"], 4)
            for t in range(TILES):
                for ct in range(CT):
                    r = slice(t * P, (t + 1) * P)
                    last = three_pass(nc, ps[:, LG, t * E:(t + 1) * E], m.xt_hi[:, ct, r], m.xt_lo[:, ct, r],
                                      m.sn_hi[:, ct], m.sn_lo[:, ct], ct == 0, ct == CT - 1)
            last.then_inc(q["lg"], 1)

            def mask_rows(n):
                h, e = divmod(n, E)
                if n >= 2:
                    pe.wait_ge(q["xm"], 2 * (n - 1))
                for t in range(4):
                    last = nc.tensor.matmul(ps[:, MB[n % 2], t * P:(t + 1) * P], m16[:, 4 * h + t, e:e + 1].to_broadcast([P, P]),
                                            m.ident16[:], start=True, stop=True)
                last.then_inc(q["mb"], 1)

            def values(h):
                pe.wait_ge(q["ev"], 3 * h + 3)
                for t in range(4):
                    last = nc.tensor.transpose(ps[:, XB[h], t * P:(t + 1) * P], vt[:, t * P:(t + 1) * P], m.const[:, K_ID:K_ID + P])
                last.then_inc(q["vt"], 1)

            pe.wait_ge(q["m"], 1)
            mask_rows(0)
            for n in range(2 * E):
                h, e = divmod(n, E)
                if n + 1 < 2 * E:
                    mask_rows(n + 1)
                pe.wait_ge(q["xm"], 2 * n + 2)
                if n == E:
                    pe.wait_ge(q["ev"], 3)
                for i in range(3):
                    for ct in range(CT):
                        last = three_pass(nc, ps[:, QB[i], :], m.w_hi[:, i, e * CT + ct], m.w_lo[:, i, e * CT + ct],
                                          xmh[:, n % XM, ct], xml[:, n % XM, ct], e == 0 and ct == 0, e == E - 1 and ct == CT - 1)
                last.then_inc(q["qkv"], 1)
                if n == E:
                    values(0)
            values(1)
            pe.wait_ge(q["v"], 2)

            def outputs(j):
                for ep in range(4):
                    z = 4 * j + ep
                    if z >= 2:
                        pe.wait_ge(q["z"], 2 * (z - 1))
                    r, c = slice(j * P, (j + 1) * P), slice(2 * ep * C, (2 * ep + 2) * C)
                    three_pass(nc, ps[:, ZB[z % 2], :], at_hi[:, r], at_lo[:, r], m.o_hi[:, c], m.o_lo[:, c], True, True).then_inc(q["zz"], 1)

            for i in turns:
                if i < TILES:
                    if i == 0:
                        pe.wait_ge(q["ev"], 6)
                    if i >= 2:
                        pe.wait_ge(q["exp"], i - 1)
                    n = (i + 1) * P
                    for a in range(0, n, HALF):
                        z = min(n, a + HALF)
                        last = nc.tensor.matmul(ps[:, SB[i % 2] + a // HALF, 0:z - a], qt[:, i * P:(i + 1) * P], kt[:, a:z],
                                                start=True, stop=True)
                    last.then_inc(q["s"], 1)
                if 0 <= i - 1 < TILES:
                    j = i - 1
                    pe.wait_ge(q["exp"], j + 1)
                    for c, (k0, k1) in enumerate(chunks(j)):
                        if before[j] + c:
                            pe.wait_ge(q["pte"], before[j] + c)
                        for k in range(k0, k1):
                            last = nc.tensor.transpose(ps[:, PB, (k - k0) * P:(k - k0 + 1) * P], pp[:, j % 2, k * P:(k + 1) * P],
                                                       m.const[:, K_ID:K_ID + P])
                        last.then_inc(q["ptc"], 1)
                if 5 <= i < 9:
                    outputs(i - 5)
                if i in (4, 8):
                    h = i // 4 - 1
                    pe.wait_ge(q["pte"], before[4 * h + 4])
                    if h:
                        pe.wait_ge(q["atl"], 1)
                    keys = 4 * h + 4
                    for k in range(keys):
                        q0 = max(0, k - 4 * h) * P
                        last = nc.tensor.matmul(ps[:, AB, q0:HALF], vv[:, k, :], pt[:, k, q0:HALF], start=k == 0, stop=k == keys - 1)
                    last.then_inc(q["pv"], 1)
                if i >= 9:
                    pe.wait_ge(q["atl"], 2)
                    outputs(i - 5)
                elif i == 4:
                    pe.wait_ge(q["atl"], 1)


ATT_SEMS = ("chain pchain achain var rstd u ss rs xn tr hi lo lat pj qkv sqd rsq nsq rq qn hlh hl kr va kz qtr qt kt s e msk "
            "pv at att an tr2 hi2 lo2 o r r_free")


def attention(nc, m, q, local):
    v = m.carve(("qkv", TILES * QKV, F32), ("t", 4 * QK, F32), ("rot", TILES * QK, F32),
                ("qe", 4 * H * 4 * HD, F16), ("ke", 4 * KVH * 8 * HD, F16), ("qt", TILES * S, F16), ("kz", KVH * 2 * S, F16),
                ("va", TILES * KVH * 32, F32), ("ssq", TILES * (H + KVH), F32))
    U = m.xa
    qkv = v["qkv"].rearrange("p (t n) -> p t n", t=TILES)
    rot = v["rot"].rearrange("p (t n) -> p t n", t=TILES)
    qn = v["t"][:, 0:4 * H * HD].rearrange("p (n d) -> p n d", d=HD)
    kn = v["t"][:, 4 * H * HD:].rearrange("p (n d) -> p n d", d=HD)
    qe = v["qe"].rearrange("p (n s d) -> p n s d", s=4, d=HD)
    ke = v["ke"].rearrange("p (n z s d) -> p n z s d", z=2, s=4, d=HD)
    qt = v["qt"].rearrange("p (r n) -> p r n", r=H // 2)
    kz = v["kz"].rearrange("p (g s n) -> p g s n", g=KVH, s=2)
    va = v["va"].rearrange("p (t g d) -> p t g d", t=TILES, g=KVH)
    ssq = v["ssq"].rearrange("p (t h) -> p t h", t=TILES)
    pr = m.at("pr", 0, PR * 2 * HALF).rearrange("p (r j n) -> p r j n", r=PR, j=2)
    at = m.at("at", PR * 2 * HALF, 2 * HALF).rearrange("p (r n) -> p r n", r=2)
    rc = m.at("rc", PR * 2 * HALF + 2 * HALF, 16).rearrange("p (t h) -> p t h", t=4)
    lat_t = m.at("lat", TILES * QKV + 4 * QK, S)[0:LAT, :]
    var, rstd, ss, rs = (m.small[:, i, :] for i in range(4))
    ps, ps16 = m.ps, m.ps[:].bitcast(F16)
    cos = m.const[:, K_COS + 128 * local:K_COS + 128 * local + 64].rearrange("p (t f) -> p t f", t=TILES)
    sin = m.const[:, K_COS + 128 * local + 64:K_COS + 128 * local + 128].rearrange("p (t f) -> p t f", t=TILES)
    w0 = GW if local else 0
    wo = GW + LW + (C if local else 0)
    XB, JB, LB = [0, 1], [2, 3], [4, 5]
    TB, KB = [4, 5], [6, 7]
    SB, VB, AB = [0, 2], [4, 5], 6
    OB = [0, 1]

    steps = []
    for g in range(KVH):
        if local:
            for k in range(TILES):
                steps.append((g, 0, k, None, k * P, min(SPAN, S - k * P), True))
        else:
            for h in range(2):
                for k in range(4 * h + 4):
                    for a in range(2):
                        q0 = max(k * P, h * HALF)
                        steps.append((g, h, k, a, q0, (h + 1) * HALF - q0, k >= 4 * h))
    masked = [n for n, s in enumerate(steps) if s[-1]]
    unit_ends = {}
    for n, (g, h, k, a, q0, w, diag) in enumerate(steps):
        if local:
            if k == 3:
                unit_ends.setdefault(n, []).append(2 * g)
            if k == TILES - 1:
                unit_ends.setdefault(n, []).append(2 * g + 1)
        elif k == 4 * h + 3 and a == 1:
            unit_ends.setdefault(n, []).append(2 * g + h)
    per = 1 if local else 2

    with nc.Block() as block:
        @block.gpsimd
        def _(pool):
            chain = Chain(pool, q["pchain"])
            nc.gpsimd.memset(kz[64:128, :, 0, :], 0.0).then_inc(q["kz"], 1)
            pool.wait_ge(q["kz"], 1)
            nc.gpsimd.memset(kz[0:64, :, 1, :], 0.0).then_inc(q["kz"], 1)
            pool.wait_ge(q["kz"], 2)
            chain.link(nc.gpsimd.memset(va, 0.0))
            chain.link(nc.gpsimd.memset(va[:, :, :, HD:HD + 1], 1.0))
            if not local:
                for h in range(2):
                    pool.wait_ge(q["var"], h + 1)
                    r = slice(4 * h, 4 * h + 4)
                    rsqrt_pool(nc, m, pool, chain, rstd[:, r], var[:, r], 1.0, 1e-5, m.half[:, 0:4]).then_inc(q["rstd"], 1)
            pool.wait_ge(q["ss"], TILES)
            rsqrt_pool(nc, m, pool, chain, rs, ss, 1.0 / C, 1e-6, m.half[:, 0:TILES]).then_inc(q["rs"], 1)
            for h in range(2):
                r = slice(4 * h, 4 * h + 4)
                pool.wait_ge(q["qkv"], 4 * h + 4)
                nc.gpsimd.tensor_copy(va[:, r, :, 0:HD], qkv[:, r, QK:].rearrange("p t (g d) -> p t g d", d=HD)).then_inc(q["va"], 1)
                pool.wait_ge(q["nsq"], h + 1)
                sr = ssq[:, r, :].rearrange("p t h -> p (t h)")
                rsqrt_pool(nc, m, pool, chain, sr, sr, 1.0 / HD, 1e-6, m.half[:, 0:4 * (H + KVH)]).then_inc(q["rq"], 1)

        @block.vector
        def _(dve):
            chain = Chain(dve, q["chain"])
            if not local:
                layernorm(nc, m, dve, chain, q, m.xb, lambda h: None)
                for h in range(2):
                    dve.wait_ge(q["rstd"], h + 1)
                    for t in range(4 * h, 4 * h + 4):
                        nc.vector.tensor_scalar(U[:, t, :], m.xb[:, t, :], m.mv[:, t, 0:1], rstd[:, t:t + 1],
                                                ALU.subtract, ALU.mult).then_inc(q["u"], 1)
                dve.wait_ge(q["u"], TILES)
            dve.wait_ge(q["rs"], 1)
            for t in range(TILES):
                nc.vector.tensor_scalar(m.xn[:, t, :], U[:, t, :], rs[:, t:t + 1], None, ALU.mult).then_inc(q["xn"], 1)
            for n in range(4):
                h, ct = divmod(n, 2)
                r = slice(h * HALF, (h + 1) * HALF)
                dve.wait_ge(q["hi"], n + 1)
                nc.vector.tensor_tensor(m.xt_lo[:, ct, r], ps[:, XB[ct], :], m.xt_hi[:, ct, r].bitcast(F32),
                                        ALU.subtract).then_inc(q["lo"], 1)
            for h in range(2):
                r = slice(4 * h, 4 * h + 4)
                hs = H + KVH
                shape = [P, 4, hs, HD // 2]
                pair = qkv[:, r, 0:QK].rearrange("p t (h f z) -> p t h f z", h=hs, z=2)
                to = rot[:, r, :].rearrange("p t (h f z) -> p t h f z", h=hs, z=2)
                even, odd = pair[:, :, :, :, 0], pair[:, :, :, :, 1]
                cb, sb_ = (x[:, r, :].unsqueeze(2).to_broadcast(shape) for x in (cos, sin))
                t1 = v["t"][:, 0:2 * QK].rearrange("p (t h f) -> p t h f", t=4, h=hs)
                t2 = v["t"][:, 2 * QK:].rearrange("p (t h f) -> p t h f", t=4, h=hs)
                dve.wait_ge(q["qkv"], 4 * h + 4)
                if h == 0 and not local:
                    dve.wait_ge(q["pj"], TILES)
                if h == 1:
                    dve.wait_ge(q["hl"], 3)
                chain.done(nc.vector.tensor_tensor(t1, even, cb, ALU.mult))
                chain.link(nc.vector.tensor_tensor(t2, odd, sb_, ALU.mult))
                chain.link(nc.vector.tensor_tensor(to[:, :, :, :, 0], t1, t2, ALU.subtract))
                chain.done(nc.vector.tensor_tensor(t1, even, sb_, ALU.mult))
                chain.link(nc.vector.tensor_tensor(t2, odd, cb, ALU.mult))
                nc.vector.tensor_tensor(to[:, :, :, :, 1], t1, t2, ALU.add).then_inc(q["rsq"], 1)
                sqv = v["t"].rearrange("p (n d) -> p n d", d=HD)
                dve.wait_ge(q["sqd"], h + 1)
                nc.vector.tensor_reduce(ssq[:, r, :].rearrange("p t h -> p (t h)"), sqv, AX.X, ALU.add).then_inc(q["nsq"], 1)
                dve.wait_ge(q["rq"], h + 1)
                for o, h0, hn in ((qn, 0, H), (kn, H, KVH)):
                    shape = [P, 4, hn, HD]
                    nc.vector.tensor_tensor(o.rearrange("p (t h) d -> p t h d", t=4),
                                            rot[:, r, h0 * HD:(h0 + hn) * HD].rearrange("p t (h d) -> p t h d", d=HD),
                                            ssq[:, r, h0:h0 + hn].unsqueeze(3).to_broadcast(shape), ALU.mult).then_inc(q["qn"], 1)
                dve.wait_ge(q["hlh"], 3 * (h + 1))
                nc.vector.tensor_tensor(qe[:, :, 1::2, :], qn.unsqueeze(2).to_broadcast([P, 4 * H, 2, HD]), qe[:, :, 0::2, :],
                                        ALU.subtract).then_inc(q["hl"], 1)
                for z in range(2):
                    nc.vector.tensor_tensor(ke[:, :, z, 2:4, :], kn.unsqueeze(2).to_broadcast([P, 4 * KVH, 2, HD]),
                                            ke[:, :, z, 0:2, :], ALU.subtract).then_inc(q["hl"], 1)
                for t in range(4 * h, 4 * h + 4):
                    dve.wait_ge(q["qtr"], t + 1)
                    nc.vector.tensor_copy(qt[:, :, t * P:(t + 1) * P],
                                          ps16[:, TB[t % 2], :].rearrange("p (r n) -> p r n", n=P)).then_inc(q["qt"], 1)

            def unit_out(n):
                g, h = divmod(n, 2)
                dve.wait_ge(q["pv"], n + 1)
                nc.vector.tensor_copy(at[:, n % 2], ps[:, VB[n % 2], :]).then_inc(q["at"], 1)

            def unit_norm(n):
                g, h = divmod(n, 2)
                dve.wait_ge(q["att"], n + 1)
                a = ps[:, AB, :].rearrange("p (t h d) -> p t h d", t=4, h=4)
                chain.link(nc.vector.reciprocal(rc, a[:, :, :, HD]))
                nc.vector.tensor_tensor(m.xn[:, 4 * h:4 * h + 4, g * 64:(g + 1) * 64].rearrange("p t (h d) -> p t h d", d=HD),
                                        a[:, :, :, 0:HD], rc.unsqueeze(3).to_broadcast([P, 4, 4, HD]), ALU.mult).then_inc(q["an"], 1)

            for n, (g, h, k, a, q0, w, diag) in enumerate(steps):
                if diag:
                    dve.wait_ge(q["e"], n + 1)
                    if local:
                        t_ = pr[:, n % PR, :, 0:2 * w].rearrange("p a (j n) -> p a j n", j=2)
                        mk = m.const[:, K_WIN:K_WIN + w].unsqueeze(1).unsqueeze(1).to_broadcast([P, 2, 2, w])
                    else:
                        t_ = pr[:, n % PR, :, 0:P]
                        mk = m.const[:, K_TRI:K_TRI + P].unsqueeze(1).to_broadcast([P, 2, P])
                    nc.vector.tensor_tensor(t_, t_, mk, ALU.mult).then_inc(q["msk"], 1)
                for u in unit_ends.get(n, ()):
                    if u >= 1:
                        unit_norm(u - 1)
                    unit_out(u)
            unit_norm(2 * KVH - 1)
            for n in range(4):
                h, ct = divmod(n, 2)
                r = slice(h * HALF, (h + 1) * HALF)
                dve.wait_ge(q["hi2"], n + 1)
                nc.vector.tensor_tensor(m.xt_lo[:, ct, r], ps[:, 6 + ct, :], m.xt_hi[:, ct, r].bitcast(F32),
                                        ALU.subtract).then_inc(q["lo2"], 1)
            for t in range(TILES):
                dve.wait_ge(q["o"], t + 1)
                add = nc.vector.tensor_tensor(U[:, t, :], U[:, t, :], ps[:, OB[t % 2], 0:C], ALU.add)
                add.then_inc(q["r"], 1)
                if local:
                    dve.wait_ge(q["r"], t + 1)
                    nc.vector.tensor_tensor(m.xb[:, t, :], m.xb[:, t, :], U[:, t, :], ALU.add)

        @block.scalar
        def _(act):
            for t in range(TILES):
                if not local:
                    act.wait_ge(q["u"], t + 1)
                if t:
                    act.wait_ge(q["ss"], t)
                nc.scalar.activation(v["t"][:, 0:C], U[:, t, :], ACT.Square, accum_out=ss[:, t:t + 1]).then_inc(q["ss"], 1)
            for n in range(4):
                h, ct = divmod(n, 2)
                act.wait_ge(q["tr"], n + 1)
                nc.scalar.copy(m.xt_hi[:, ct, h * HALF:(h + 1) * HALF], ps[:, XB[ct], :]).then_inc(q["hi"], 1)
            if not local:
                for h in range(2):
                    act.wait_ge(q["lat"], h + 1)
                    nc.scalar.copy(lat_t[:, h * HALF:(h + 1) * HALF], ps[0:LAT, LB[h], :]).then_inc(q["achain"], 1)
            for t in range(TILES):
                act.wait_ge(q["pj"], t + 1)
                nc.scalar.copy(qkv[:, t, :], ps[:, JB[t % 2], 0:QKV]).then_inc(q["qkv"], 1)
            for h in range(2):
                r = slice(4 * h, 4 * h + 4)
                act.wait_ge(q["rsq"], h + 1)
                nc.scalar.activation(v["t"].rearrange("p (t n) -> p t n", t=4), rot[:, r, :], ACT.Square).then_inc(q["sqd"], 1)
                act.wait_ge(q["qn"], 2 * (h + 1))
                if h:
                    act.wait_ge(q["qtr"], 4)
                nc.scalar.copy(qe[:, :, 0::2, :], qn.unsqueeze(2).to_broadcast([P, 4 * H, 2, HD])).then_inc(q["hlh"], 1)
                for z in range(2):
                    nc.scalar.copy(ke[:, :, z, 0:2, :], kn.unsqueeze(2).to_broadcast([P, 4 * KVH, 2, HD])).then_inc(q["hlh"], 1)
                if h == 0:
                    act.wait_ge(q["kz"], 2)
                for t in range(4 * h, 4 * h + 4):
                    act.wait_ge(q["qtr"], t + 1)
                    kp = ps16[:, KB[t % 2], 0:HALF].rearrange("p (g n) -> p g n", n=P)
                    for s in range(2):
                        half = slice(64 * s, 64 * s + 64)
                        nc.scalar.copy(kz[half, :, s, t * P:(t + 1) * P], kp[half]).then_inc(q["kt"], 1)
            for n, (g, h, k, a, q0, w, diag) in enumerate(steps):
                act.wait_ge(q["s"], n + 1)
                if n >= PR:
                    act.wait_ge(q["r_free"], n - PR + 1)
                if n == 0:
                    act.wait_ge(q["hl"], 6)
                    act.wait_ge(q["va"], 2)
                w_ = 2 * w if local else w
                nc.scalar.activation(pr[:, n % PR, :, 0:w_], ps[:, SB[n % 2]:SB[n % 2] + 2, 0:w_], ACT.Exp,
                                     scale=float(HD) ** -0.5).then_inc(q["e"], 1)
            for n in range(4):
                h, ct = divmod(n, 2)
                act.wait_ge(q["tr2"], n + 1)
                nc.scalar.copy(m.xt_hi[:, ct, h * HALF:(h + 1) * HALF], ps[:, 6 + ct, :]).then_inc(q["hi2"], 1)

        @block.tensor
        def _(pe):
            for n in range(4):
                h, ct = divmod(n, 2)
                pe.wait_ge(q["xn"], 4 * h + 4)
                if n >= 2:
                    pe.wait_ge(q["lo"], n - 1)
                transpose_rows(nc, m, pe, m.xn, h, ct, XB[ct]).then_inc(q["tr"], 1)
            pe.wait_ge(q["lo"], 4)
            if not local:
                for h in range(2):
                    r = slice(h * HALF, (h + 1) * HALF)
                    for ct in range(CT):
                        last = three_pass(nc, ps[:, LB[h], :], m.a_hi[:, ct, 0:P], m.a_lo[:, ct, 0:P], m.xt_hi[:, ct, r],
                                          m.xt_lo[:, ct, r], ct == 0, ct == CT - 1)
                    last.then_inc(q["lat"], 1)
            for t in range(TILES):
                r = slice(t * P, (t + 1) * P)
                if t >= 2:
                    pe.wait_ge(q["qkv"], t - 1)
                c0, n = (GW, QKV) if local else (LAT, H * HD)
                for ct in range(CT):
                    last = three_pass(nc, ps[:, JB[t % 2], 0:n], m.xt_hi[:, ct, r], m.xt_lo[:, ct, r],
                                      m.a_hi[:, ct, c0:c0 + n], m.a_lo[:, ct, c0:c0 + n], ct == 0, ct == CT - 1)
                if not local:
                    pe.wait_ge(q["achain"], t // 4 + 1)
                    last = nc.tensor.matmul(ps[:, JB[t % 2], n:QKV], lat_t[:, r], m.kv_up[:], start=True, stop=True)
                last.then_inc(q["pj"], 1)
            for t in range(TILES):
                pe.wait_ge(q["hl"], 3 * (t // 4 + 1))
                if t >= 2:
                    pe.wait_ge(q["qt"], t - 1)
                    pe.wait_ge(q["kt"], 2 * (t - 1))
                for j in range(H // 2):
                    src = qe[:, (t % 4) * H + 2 * j:(t % 4) * H + 2 * j + 2].rearrange("p h s d -> p (h s d)")
                    nc.tensor.transpose(ps16[:, TB[t % 2], j * P:(j + 1) * P], src, m.ident16[:])
                for g in range(KVH):
                    src = ke[:, (t % 4) * KVH + g].rearrange("p z s d -> p (z s d)")
                    last = nc.tensor.transpose(ps16[:, KB[t % 2], g * P:(g + 1) * P], src, m.ident16[:])
                last.then_inc(q["qtr"], 1)
            pe.wait_ge(q["qt"], TILES)
            pe.wait_ge(q["kt"], 2 * TILES)
            pe.wait_ge(q["va"], 2)

            def scores(n):
                g, h, k, a, q0, w, diag = steps[n]
                if n >= 2:
                    pe.wait_ge(q["e"], n - 1)
                for a_ in ((0, 1) if local else (a,)):
                    for j in range(2):
                        bank, c = (SB[n % 2] + a_, j * w) if local else (SB[n % 2] + j, 0)
                        last = nc.tensor.matmul(ps[:, bank, c:c + w], kz[:, g, j, k * P:(k + 1) * P],
                                                qt[:, 2 * g + a_, q0:q0 + w], start=True, stop=True)
                last.then_inc(q["s"], 1)

            def free_bank(u):
                if u >= 2:
                    pe.wait_ge(q["at"], u - 1)

            def products(n0):
                g, h, k, a, q0, w, diag = steps[n0]
                n1 = n0 + per - 1
                pe.wait_ge(q["e"], n1 + 1)
                masks = sum(1 for x in masked if x <= n1)
                if diag:
                    pe.wait_ge(q["msk"], masks)
                val = va[:, k, g, :]
                if local:
                    if k == 0:
                        for u in (2 * g, 2 * g + 1):
                            free_bank(u)
                            nc.tensor.matmul(ps[:, VB[u % 2], :], m.zeros16[:, 0:P], m.zeros16[:], start=True, stop=True)
                    pieces = [(q0, min(q0 + w, HALF))] if q0 < HALF else [(q0, q0 + w)]
                    if q0 < HALF < q0 + w:
                        pieces.append((HALF, q0 + w))
                    for a0, a1 in pieces:
                        for hd in range(4):
                            x = pr[:, n0 % PR, hd // 2, (hd % 2) * w + a0 - q0:(hd % 2) * w + a1 - q0]
                            last = nc.tensor.matmul(ps[32 * hd:32 * hd + 32, VB[a0 // HALF], a0 % HALF:a0 % HALF + a1 - a0], val, x,
                                                    start=False, stop=True, skip_group_check=True)
                else:
                    u = 2 * g + h
                    if k == 0:
                        free_bank(u)
                    for hd in range(4):
                        x = pr[:, (n0 + hd // 2) % PR, hd % 2, 0:w]
                        last = nc.tensor.matmul(ps[32 * hd:32 * hd + 32, VB[u % 2], q0 - h * HALF:HALF], val, x,
                                                start=k == 0, stop=k == 4 * h + 3)
                return last

            def turn(u):
                pe.wait_ge(q["at"], u + 1)
                if u:
                    pe.wait_ge(q["an"], u)
                for t in range(4):
                    last = nc.tensor.transpose(ps[:, AB, t * P:(t + 1) * P], at[:, u % 2, t * P:(t + 1) * P], m.const[:, K_ID:K_ID + P])
                last.then_inc(q["att"], 1)

            pending = []
            N = len(steps)
            for n in range(0, N + per, per):
                for i in range(n, min(n + per, N)):
                    scores(i)
                if n >= per:
                    last = products(n - per)
                    last.then_inc(q["r_free"], per)
                    while pending:
                        turn(pending.pop(0))
                    for u in unit_ends.get(n - 1, ()):
                        pending.append(u)
                        pe.wait_ge(q["r_free"], n)
                        pe.sem_inc(q["pv"], 1)
            while pending:
                turn(pending.pop(0))
            pe.wait_ge(q["an"], 2 * KVH)
            for n in range(4):
                h, ct = divmod(n, 2)
                if n >= 2:
                    pe.wait_ge(q["lo2"], n - 1)
                transpose_rows(nc, m, pe, m.xn, h, ct, 6 + ct).then_inc(q["tr2"], 1)
            pe.wait_ge(q["lo2"], 4)
            for t in range(TILES):
                r = slice(t * P, (t + 1) * P)
                if t >= 2:
                    pe.wait_ge(q["r"], t - 1)
                for ct in range(CT):
                    last = three_pass(nc, ps[:, OB[t % 2], 0:C], m.xt_hi[:, ct, r], m.xt_lo[:, ct, r],
                                      m.a_hi[:, ct, wo:wo + C], m.a_lo[:, ct, wo:wo + C], ct == 0, ct == CT - 1)
                last.then_inc(q["o"], 1)


def build(nc, ins, out):
    ctx = ExitStack()
    with ctx:
        m = Mem(nc, ctx)
        qs = semaphores(nc, ctx, "setup", SETUP_SEMS)
        qf, qa = semaphores(nc, ctx, "ffn", FFN_SEMS), semaphores(nc, ctx, "att", ATT_SEMS)
        x = ins["L0_attn_hidden"]
        setup(nc, m, qs, ins)
        with nc.Fori(0, B) as b:
            ffn(nc, m, qf, b, x, out, True)
            clear(nc, qf)
            for local in (False, True):
                attention(nc, m, qa, local)
                clear(nc, qa)
            ffn(nc, m, qf, b, x, out, False)
            clear(nc, qf)


_INS = ["L0_attn_hidden", "L0_attn_norm1_w", "L0_attn_norm2_w", "L0_attn_g_wq", "L0_attn_g_kv_down", "L0_attn_g_k_up",
        "L0_attn_g_v_up", "L0_attn_g_wo", "L0_attn_l_wq", "L0_attn_l_wk", "L0_attn_l_wv", "L0_attn_l_wo", "L0_ffn_sim_matrix",
        "L0_ffn_gates", "L0_ffn_q_proj", "L0_ffn_k_proj", "L0_ffn_v_proj", "L0_ffn_o_proj"]


def constants():
    import numpy as np
    c = np.zeros((P, K_ALL), np.float32)
    i, j = np.arange(P)[:, None], np.arange(P)[None, :]
    c[:, K_ID:K_ID + P] = i == j
    c[:, K_NEG:K_NEG + P] = np.where(j > i, -1e30, 0.0)
    c[:, K_TRI:K_TRI + P] = j >= i
    d = np.arange(SPAN)[None, :] - i
    c[:, K_WIN:K_WIN + SPAN] = (d >= 0) & (d < WIN)
    e = np.arange(E)
    c[:, K_TRI8:K_TRI8 + E * E] = (e[None, :] < e[:, None]).astype(np.float32).reshape(1, -1)
    for n, base in enumerate((1000000.0, 10000.0)):
        inv = (np.float32(1.0) / np.float32(base) ** (np.arange(0, HD, 2, dtype=np.float32) / np.float32(HD))).astype(np.float32)
        f = (np.arange(S, dtype=np.float32)[:, None] * inv[None, :]).reshape(TILES, P, HD // 2).transpose(1, 0, 2).reshape(P, 64)
        c[:, K_COS + 128 * n:K_COS + 128 * n + 64] = np.cos(f)
        c[:, K_COS + 128 * n + 64:K_COS + 128 * n + 128] = np.sin(f)
    return c


def kernel(**inputs):
    import numpy as np
    import concourse.bacc as bacc
    from concourse.bass_utils import run_bass_kernel_spmd

    nc = bacc.Bacc("TRN2", target_bir_lowering=False, num_devices=1)
    arrays, ins = {}, {}
    for name in _INS:
        a = np.ascontiguousarray(inputs[name])
        arrays[f"in_{name}"] = a
        ins[name] = nc.dram_tensor(f"in_{name}", a.shape, mybir.dt.from_np(a.dtype), kind="ExternalInput").ap()
    arrays["in_const"] = constants()
    ins["const"] = nc.dram_tensor("in_const", (P, K_ALL), F32, kind="ExternalInput").ap()
    out = nc.dram_tensor("out_dram", (B, S, C), F32, kind="ExternalOutput").ap()
    build(nc, ins, out)
    r = run_bass_kernel_spmd(nc, [arrays], core_ids=[0])
    return r.results[0]["out_dram"]
```

```python
import concourse.bass as bass
from concourse import mybir
from contextlib import ExitStack

P = 128
B, S, C = 4, 1024, 256
TILES = S // P
CT = C // P
HALF = 512
E, D = 8, 128
H, KVH, HD = 16, 4, 16
LAT = 64
WIN = 64
QK = (H + KVH) * HD
QKV = QK + KVH * HD
GW = LAT + H * HD
LW = QKV
AW = GW + LW + 2 * C
SPAN = P + WIN
XM = 4
PR = 6
LAG = 2
MASKED = -30000.0

K_ID, K_NEG, K_WIN, K_TRI8, K_COS = 0, 128, 256, 256 + SPAN, 256 + SPAN + 64
K_TRI = K_COS + 4 * 64
K_ALL = K_TRI + 128

F32, F16, F32R, I32 = mybir.dt.float32, mybir.dt.float16, mybir.dt.float32r, mybir.dt.int32
ALU, ACT, AX = mybir.AluOpType, mybir.ActivationFunctionType, mybir.AxisListType


class Mem:

    def __init__(self, nc, ctx):
        def sb(name, shape, dt=F32):
            return ctx.enter_context(nc.sbuf_tensor(name, shape, dt))
        self.const = sb("const", [P, K_ALL])
        self.ident16 = sb("ident16", [P, P], F16)
        self.zeros16 = sb("zeros16", [P, P], F16)
        self.win16 = sb("win16", [P, 2, SPAN], F16)
        self.tri16 = sb("tri16", [P, P], F16)
        self.w_hi = sb("w_hi", [P, 3, E * CT, D], F32R)
        self.w_lo = sb("w_lo", [P, 3, E * CT, D], F32R)
        self.o_hi = sb("o_hi", [P, E * C], F32R)
        self.o_lo = sb("o_lo", [P, E * C], F32R)
        self.a_hi = sb("a_hi", [P, CT, AW], F32R)
        self.a_lo = sb("a_lo", [P, CT, AW], F32R)
        self.kv_up = sb("kv_up", [LAT, 2 * KVH * HD])
        self.sn_hi = sb("sn_hi", [P, CT, E], F32R)
        self.sn_lo = sb("sn_lo", [P, CT, E], F32R)
        self.sig = sb("sig", [P, E])
        self.norm_w = sb("norm_w", [P, 2, CT])
        self.xa = sb("xa", [P, TILES, C])
        self.xb = sb("xb", [P, TILES, C])
        self.xn = sb("xn", [P, TILES, C])
        self.xt_hi = sb("xt_hi", [P, CT, S], F32R)
        lo_base = nc.sbuf_base
        self.xt_lo = sb("xt_lo", [P, CT, S], F32R)
        self.stats = sb("stats", [P, TILES, 6])
        self.mv = sb("mv", [P, TILES, 2])
        self.small = sb("small", [P, 8, TILES])
        self.rc = sb("rc", [P, 16])
        self.arena_bytes = 78 * 1024
        self.nc, self.base, self.views = nc, nc.sbuf_base, 0
        sb("arena", [P, self.arena_bytes // 4])
        self.at_xt_lo = nc.alloc_sbuf_tensor_at("at_xt_lo", [P, CT, S], F32, offset=lo_base, align_bytes=4)
        self.ps = ctx.enter_context(nc.psum_tensor("ps", [P, 8, HALF], F32))

    def at(self, name, word, n, dt=F32):
        words = n // 2 if dt == F16 else n
        assert (word + words) * 4 <= self.arena_bytes, (name, word + words)
        self.views += 1
        return self.nc.alloc_sbuf_tensor_at(f"{name}_{self.views}", [P, n], dt, offset=self.base + 4 * word, align_bytes=4)[:]

    def carve(self, *parts):
        word, views = 0, {}
        for name, n, dt in parts:
            views[name] = self.at(name, word, n, dt)
            word += n // 2 if dt == F16 else n
        return views


class Chain:

    def __init__(self, eng, sem):
        self.eng, self.sem, self.n = eng, sem, 0

    def done(self, ins):
        self.n += 1
        ins.then_inc(self.sem, 1)

    def wait(self):
        self.eng.wait_ge(self.sem, self.n)

    def link(self, ins):
        self.done(ins)
        self.wait()


def semaphores(nc, ctx, stage, names):
    return {name: ctx.enter_context(nc.semaphore(f"{stage}_{name}")) for name in names.split()}


def rsqrt(nc, chain, out, t, x):
    chain.link(nc.vector.tensor_scalar(t.bitcast(I32), x.bitcast(I32), 1, None, ALU.logical_shift_right))
    chain.link(nc.vector.tensor_scalar(out.bitcast(I32), t.bitcast(I32), -1.0, float(0x5F3759DF), ALU.mult, ALU.add))
    for _ in range(3):
        chain.link(nc.vector.scalar_tensor_tensor(t, out, -0.5, out, ALU.mult, ALU.mult))
        chain.link(nc.vector.tensor_tensor(t, t, x, ALU.mult))
        last = nc.vector.scalar_tensor_tensor(out, t, 1.5, out, ALU.add, ALU.mult)
        chain.link(last)


SETUP_SEMS = "const w oo aw misc cast stage hi chain pchain pre sq exp"


def setup(nc, m, q, ins):
    v = m.carve(("wst", 3 * E * CT * D, F32), ("ost", E * C, F32), ("ast", CT * AW, F32),
                ("sim", CT * E, F32), ("sq", CT * E, F32), ("ones", P, F32), ("gt", E, F32), ("rn", E, F32), ("rt", E, F32))
    wst = v["wst"].rearrange("p (w k d) -> p w k d", w=3, d=D)
    ast = v["ast"].rearrange("p (t n) -> p t n", t=CT)
    sim = v["sim"].rearrange("p (t e) -> p t e", t=CT)
    sq = v["sq"].rearrange("p (t e) -> p t e", t=CT)
    ones, gt, rn, rt = v["ones"], v["gt"], v["rn"], v["rt"]
    norm_ps = m.ps[:, 0, 0:E]

    with nc.Block() as block:
        @block.sync
        def _(sp):
            sp.dma_start(m.const[:], ins["const"]).then_inc(q["const"], 16)
            sp.dma_start(sim, ins["L0_ffn_sim_matrix"].rearrange("(t p) e -> p t e", p=P)).then_inc(q["misc"], 16)
            sp.dma_start(m.norm_w[:, 0, :], ins["L0_attn_norm1_w"].rearrange("(t p) -> p t", p=P),
                         allow_slow_non_contiguous=True).then_inc(q["misc"], 16)
            sp.dma_start(m.norm_w[:, 1, :], ins["L0_attn_norm2_w"].rearrange("(t p) -> p t", p=P),
                         allow_slow_non_contiguous=True).then_inc(q["misc"], 16)
            sp.dma_start(gt, ins["L0_ffn_gates"].partition_broadcast(P)).then_inc(q["misc"], 16)
            for i, n in enumerate(("q", "k", "v")):
                sp.dma_start(wst[:, i], ins[f"L0_ffn_{n}_proj"].rearrange("e (t p) d -> p (e t) d", p=P)).then_inc(q["w"], 16)
            sp.dma_start(v["ost"].rearrange("p (e c) -> p e c", e=E),
                         ins["L0_ffn_o_proj"].rearrange("e d c -> d e c")).then_inc(q["oo"], 16)

        @block.gpsimd
        def _(pool):
            chain = Chain(pool, q["pchain"])
            chain.done(nc.gpsimd.memset(m.zeros16[:], 0.0))
            nc.gpsimd.memset(ones, 1.0).then_inc(q["pre"], 1)

        @block.tensor
        def _(pe):
            pe.wait_ge(q["pre"], 1)
            pe.wait_ge(q["sq"], 1)
            for t in range(CT):
                ins_ = nc.tensor.matmul(norm_ps, ones, sq[:, t], start=t == 0, stop=t == CT - 1)
            ins_.then_inc(q["stage"], 1)

        @block.scalar
        def _(act):
            at = 0
            for name, n in (("L0_attn_g_kv_down", LAT), ("L0_attn_g_wq", C), ("L0_attn_l_wq", C), ("L0_attn_l_wk", KVH * HD),
                            ("L0_attn_l_wv", KVH * HD), ("L0_attn_g_wo", C), ("L0_attn_l_wo", C)):
                act.dma_start(ast[:, :, at:at + n], ins[name].rearrange("(t p) n -> p t n", p=P)).then_inc(q["aw"], 16)
                at += n
            act.dma_start(m.kv_up[:, 0:KVH * HD], ins["L0_attn_g_k_up"]).then_inc(q["aw"], 16)
            act.dma_start(m.kv_up[:, KVH * HD:], ins["L0_attn_g_v_up"]).then_inc(q["aw"], 16)
            act.wait_ge(q["misc"], 64)
            nc.scalar.activation(gt, gt, ACT.Exp, scale=-1.0).then_inc(q["exp"], 1)
            act.wait_ge(q["w"], 48)
            nc.scalar.copy(m.w_hi[:], wst).then_inc(q["hi"], 1)
            act.wait_ge(q["oo"], 16)
            nc.scalar.copy(m.o_hi[:], v["ost"]).then_inc(q["hi"], 1)
            act.wait_ge(q["cast"], 4)
            nc.scalar.copy(m.a_hi[:], ast).then_inc(q["hi"], 1)

        @block.vector
        def _(dve):
            chain = Chain(dve, q["chain"])
            dve.wait_ge(q["misc"], 64)
            nc.vector.tensor_tensor(sq, sim, sim, ALU.mult).then_inc(q["sq"], 1)
            dve.wait_ge(q["const"], 16)
            nc.vector.tensor_copy(m.ident16[:], m.const[:, K_ID:K_ID + P])
            for j in range(2):
                nc.vector.tensor_scalar(m.win16[:, j, :], m.const[:, K_WIN:K_WIN + SPAN], -MASKED, MASKED, ALU.mult, ALU.add)
            nc.vector.tensor_scalar(m.tri16[:], m.const[:, K_TRI:K_TRI + P], -MASKED, MASKED, ALU.mult, ALU.add)
            dve.wait_ge(q["exp"], 1)
            chain.link(nc.vector.tensor_scalar(gt, gt, 1.0, None, ALU.add))
            chain.link(nc.vector.reciprocal(m.sig[:], gt))
            dve.wait_ge(q["stage"], 1)
            chain.link(nc.vector.tensor_scalar(gt, norm_ps, 1e-24, None, ALU.max))
            rsqrt(nc, chain, rn, rt, gt)
            dve.wait_ge(q["aw"], 16 * 9)
            for t in range(CT):
                for i, (a, n) in enumerate(((0, GW), (GW, LW))):
                    nc.vector.tensor_scalar(ast[:, t, a:a + n], ast[:, t, a:a + n], m.norm_w[:, i, t:t + 1], None,
                                            ALU.mult).then_inc(q["cast"], 1)
            chain.link(nc.vector.tensor_tensor(sim, sim, rn.unsqueeze(1).to_broadcast([P, CT, E]), ALU.mult))
            chain.link(nc.vector.tensor_copy(m.sn_hi[:], sim))
            chain.done(nc.vector.tensor_tensor(m.sn_lo[:], sim, m.sn_hi[:].bitcast(F32), ALU.subtract))
            dve.wait_ge(q["hi"], 1)
            nc.vector.tensor_tensor(m.w_lo[:], wst, m.w_hi[:].bitcast(F32), ALU.subtract)
            dve.wait_ge(q["hi"], 2)
            nc.vector.tensor_tensor(m.o_lo[:], v["ost"], m.o_hi[:].bitcast(F32), ALU.subtract)
            dve.wait_ge(q["hi"], 3)
            nc.vector.tensor_tensor(m.a_lo[:], ast, m.a_hi[:].bitcast(F32), ALU.subtract)


def clear(nc, q):
    ids = [s.num for s in q.values()]
    assert max(ids) - min(ids) == len(ids) - 1
    nc.gpsimd.sem_clear(range(min(ids), max(ids) + 1))
    nc.all_engine_barrier()


FFN_SEMS = ("x0 x1 chain xln tr hi lo lt ltc lg m gmax gexp mb xm qkv ev vt v s nm exp ptc pte pv ath atl "
            "zz z w2 y pchain res out")


def layernorm(nc, m, dve, chain, x, out, ready, done):
    var, rstd, guess = (m.small[:, i, :] for i in (0, 1, 4))
    for h in range(2):
        ready(h)
        for t in range(4 * h, 4 * h + 4):
            chain.done(nc.vector.bn_stats(m.stats[:, t, :], x[:, t, :]))
    chain.wait()
    for t in range(TILES):
        chain.done(nc.vector.bn_aggr(m.mv[:, t, :], m.stats[:, t, :]))
    chain.wait()
    chain.link(nc.vector.tensor_scalar(var, m.mv[:, :, 1], 1e-5, None, ALU.add))
    rsqrt(nc, chain, rstd, guess, var)
    for t in range(TILES):
        done(nc.vector.tensor_scalar(out[:, t, :], x[:, t, :], m.mv[:, t, 0:1], rstd[:, t:t + 1],
                                     ALU.subtract, ALU.mult))


def normed_mean_square(nc, m, chain, out):
    rstd = m.small[:, 1, :]
    chain.link(nc.vector.tensor_tensor(out, m.mv[:, :, 1], rstd, ALU.mult))
    chain.link(nc.vector.tensor_tensor(out, out, rstd, ALU.mult))


def transpose_rows(nc, m, pe, src, h, ct, bank):
    for t in range(4):
        ins = nc.tensor.transpose(m.ps[:, bank, t * P:t * P + P], src[:, 4 * h + t, ct * P:ct * P + P],
                                  m.const[:, K_ID:K_ID + P])
    return ins


def three_pass(nc, out, w_hi, w_lo, x_hi, x_lo, first, last):
    nc.tensor.matmul(out, w_hi, x_hi, start=first, stop=False)
    nc.tensor.matmul(out, w_lo, x_hi, start=False, stop=False)
    return nc.tensor.matmul(out, w_hi, x_lo, start=False, stop=last)


def ffn(nc, m, q, b, x_dram, out_dram, first):
    x, out = (m.xa, m.xb) if first else (m.xb, m.xa)
    v = m.carve(("xmh", XM * CT * HALF, F32R), ("xml", XM * CT * HALF, F32R), ("qt", S, F32), ("kt", S, F32),
                ("vt", HALF, F32), ("v", TILES * D, F32), ("p", 2 * S, F32), ("at_hi", S, F32R), ("at_lo", S, F32R),
                ("m16", TILES * E, F16), ("lg", TILES * E, F32), ("gated", TILES * E, F32), ("mask", TILES * E, F32),
                ("w", TILES * E, F32), ("w2", TILES * E, F32), ("cnt", TILES, F32), ("rsum", TILES, F32),
                ("nmax", TILES, F32), ("rinv", TILES, F32), ("g", TILES * E * E, F32),
                ("pt0", 4 * HALF, F32))
    v["eq"] = m.at("eq", 0, TILES * E * E)
    xmh = v["xmh"].rearrange("p (r t n) -> p r t n", r=XM, t=CT)
    xml = v["xml"].rearrange("p (r t n) -> p r t n", r=XM, t=CT)
    pt = [v["pt0"].rearrange("p (k n) -> p k n", n=HALF), m.at("pt1", 0, TILES * HALF).rearrange("p (k n) -> p k n", n=HALF)]
    vv = v["v"].rearrange("p (t d) -> p t d", t=TILES)
    pp = v["p"].rearrange("p (r n) -> p r n", r=2)
    te = lambda n: v[n].rearrange("p (t e) -> p t e", t=TILES)
    m16, lg, gated, mask, w, w2 = (te(n) for n in ("m16", "lg", "gated", "mask", "w", "w2"))
    qt, kt, vt, at_hi, at_lo, cnt, rsum, nmax, rinv = (v[n] for n in
        ("qt", "kt", "vt", "at_hi", "at_lo", "cnt", "rsum", "nmax", "rinv"))
    lg_t = v["p"][0:E, 0:S]
    ps = m.ps
    ss, rn = m.small[:, 2, :], m.small[:, 3, :]
    XB = [0, 1, 4, 5]
    LT, LG = [6, 7], 2
    MB = [2, 3]
    QB = [4, 5, 6]
    VB = [0, 3]
    EARLY = 0
    AB = [7, 4]
    score_bank = lambda i: [7, 1][i % 2] if i < 4 else [4, 6][i % 2]
    probs_bank = lambda n: 0 if n < 4 else n % 2
    OB = [1, 0] * (2 * EARLY) + [2, 3] * (8 - 2 * EARLY) + [2, 3, 5, 6] * 4
    scaled = m.xn[:].rearrange("p (r e) c -> p r e c", r=2)

    def chunks(i):
        return [(k, min(k + 4, i + 1)) for k in range(0, i + 1, 4)]
    before = [sum(len(chunks(j)) for j in range(i)) for i in range(TILES + 1)]

    def scores_of(i):
        bank = score_bank(i)
        return (ps[:, bank:bank + 2, :] if i >= 4 else ps[:, bank:bank + 1, :]).rearrange("p b n -> p (b n)")

    early = {0: "v0", 1: "s0 s1", 2: "t0 s2", 3: "t1 s3", 4: "t2", 5: "t3 a0", 6: "", 7: ""}
    late = "s4 v1 s5 o0 t4 o1 s6 t5 s7 t6 o2 t7 a1 o3 o4 o5 o6 o7"

    def run(work, names):
        for name in names.split():
            if name[0] in work:
                work[name[0]](int(name[1]))

    def add_scaled(engine, eng, chain, j):
        part = scaled[:, j % 2]
        eng.wait_ge(q["y"], 4 * j + 4)
        chain.link(engine.tensor_tensor(part[:, 0:2, :], part[:, 0:2, :], part[:, 2:4, :], ALU.add))
        chain.link(engine.tensor_tensor(part[:, 0, :], part[:, 0, :], part[:, 1, :], ALU.add))
        eng.wait_ge(q["z"], 4 * j + 4)
        engine.tensor_tensor(out[:, j, :], out[:, j, :], part[:, 0, :], ALU.add).then_inc(q["res"], 1)

    with nc.Block() as block:
        @block.sync
        def _(sp):
            if first:
                for h, s in enumerate((q["x0"], q["x1"])):
                    sp.dma_start(x[:, 4 * h:4 * h + 4, :],
                                 x_dram[bass.ds(b, 1), h * HALF:(h + 1) * HALF, :].rearrange("b (t p) c -> p (b t) c", p=P)).then_inc(s, 16)
            else:
                for h in range(2):
                    sp.wait_ge(q["res"], 4 * h + 4)
                    sp.dma_start(out_dram[bass.ds(b, 1), h * HALF:(h + 1) * HALF, :].rearrange("b (t p) c -> p (b t) c", p=P),
                                 out[:, 4 * h:4 * h + 4, :]).then_inc(q["out"], 16)
                sp.wait_ge(q["out"], 32)

        @block.vector
        def _(dve):
            chain = Chain(dve, q["chain"])
            layernorm(nc, m, dve, chain, x, m.xn, (lambda h: dve.wait_ge(q[f"x{h}"], 16)) if first else (lambda h: None),
                      lambda ins: ins.then_inc(q["xln"], 1))
            normed_mean_square(nc, m, chain, ss)
            chain.link(nc.vector.tensor_scalar(ss, ss, float(C), 1e-24, ALU.mult, ALU.max))
            rsqrt(nc, chain, rn, m.small[:, 4, :], ss)
            for n in range(4):
                h, ct = divmod(n, 2)
                r = slice(h * HALF, (h + 1) * HALF)
                dve.wait_ge(q["hi"], n + 1)
                nc.vector.tensor_tensor(m.xt_lo[:, ct, r], ps[:, XB[n], :], m.xt_hi[:, ct, r].bitcast(F32),
                                        ALU.subtract).then_inc(q["lo"], 1)
            dve.wait_ge(q["lg"], 1)
            full = [P, TILES, E]
            cube = [P, TILES, E, E]
            chain.link(nc.vector.tensor_tensor(lg, ps[:, LG, 0:TILES * E].rearrange("p (t e) -> p t e", t=TILES),
                                               rn.unsqueeze(2).to_broadcast(full), ALU.mult))
            chain.link(nc.vector.tensor_tensor(lg, lg, m.sig[:].unsqueeze(1).to_broadcast(full), ALU.subtract))
            chain.done(nc.vector.tensor_scalar(gated, lg, 0.0, None, ALU.max))
            chain.done(nc.vector.tensor_scalar(mask, lg, 0.0, None, ALU.is_gt))
            g = v["g"].rearrange("p (t e j) -> p t e j", t=TILES, e=E)
            eq = v["eq"].rearrange("p (t e j) -> p t e j", t=TILES, e=E)
            le, lj = lg.unsqueeze(3).to_broadcast(cube), lg.unsqueeze(2).to_broadcast(cube)
            chain.done(nc.vector.tensor_tensor(g, lj, le, ALU.is_gt))
            chain.link(nc.vector.tensor_tensor(eq, lj, le, ALU.is_equal))
            lower = m.const[:, K_TRI8:K_TRI8 + 64].rearrange("p (e j) -> p e j", e=E).unsqueeze(1).to_broadcast(cube)
            chain.link(nc.vector.tensor_tensor(eq, eq, lower, ALU.mult))
            chain.link(nc.vector.tensor_tensor(g, g, eq, ALU.add))
            chain.done(nc.vector.tensor_reduce(w2, g, AX.X, ALU.add))
            chain.done(nc.vector.tensor_reduce(cnt, mask, AX.X, ALU.add))
            chain.link(nc.vector.tensor_reduce(nmax, gated, AX.X, ALU.max))
            chain.done(nc.vector.tensor_scalar(w2, w2, 2.0, None, ALU.is_lt))
            chain.done(nc.vector.tensor_tensor(gated, gated, nmax.unsqueeze(2).to_broadcast(full), ALU.subtract))
            chain.link(nc.vector.tensor_scalar(cnt, cnt, 0.0, None, ALU.is_equal))
            chain.link(nc.vector.tensor_tensor(w2, w2, cnt.unsqueeze(2).to_broadcast(full), ALU.mult))
            chain.link(nc.vector.tensor_tensor(mask, mask, w2, ALU.max))
            nc.vector.tensor_copy(m16, mask).then_inc(q["m"], 1)
            def routing_weights():
                dve.wait_ge(q["gexp"], 1)
                chain.link(nc.vector.tensor_tensor(w, w, mask, ALU.mult))
                chain.link(nc.vector.tensor_reduce(cnt, w, AX.X, ALU.add))
                chain.link(nc.vector.reciprocal(cnt, cnt))
                chain.link(nc.vector.tensor_scalar(cnt, cnt, 0.5, None, ALU.mult))
                chain.link(nc.vector.tensor_tensor(w, w, cnt.unsqueeze(2).to_broadcast(full), ALU.mult))

            def masked(n):
                h, e = divmod(n, E)
                r = slice(h * HALF, (h + 1) * HALF)
                dve.wait_ge(q["mb"], n + 1)
                if n >= XM:
                    dve.wait_ge(q["qkv"], n - XM + 1)
                mb = ps[:, MB[n % 2], :].unsqueeze(1).to_broadcast([P, CT, HALF])
                for o, i in ((xmh, m.xt_hi), (xml, m.xt_lo)):
                    nc.vector.tensor_tensor(o[:, n % XM], i[:, :, r].bitcast(F32), mb, ALU.mult).then_inc(q["xm"], 1)

            def row_max(i):
                dve.wait_ge(q["s"], i + 1)
                sc = scores_of(i)
                dg = sc[:, i * P:(i + 1) * P]
                chain.link(nc.vector.tensor_tensor(dg, dg, m.const[:, K_NEG:K_NEG + P], ALU.add))
                nc.vector.tensor_reduce(nmax[:, i:i + 1], sc[:, 0:(i + 1) * P], AX.X, ALU.max, negate=True).then_inc(q["nm"], 1)

            def take_probs(j):
                for c, (k0, k1) in enumerate(chunks(j)):
                    n = before[j] + c
                    dve.wait_ge(q["ptc"], n + 1)
                    nc.vector.tensor_copy(pt[j // 4][:, k0:k1, (j % 4) * P:(j % 4 + 1) * P],
                                          ps[:, probs_bank(n), 0:(k1 - k0) * P].rearrange("p (k n) -> p k n", n=P)).then_inc(q["pte"], 1)

            def attended_low(h):
                dve.wait_ge(q["ath"], h + 1)
                r = slice(h * HALF, (h + 1) * HALF)
                nc.vector.tensor_tensor(at_lo[:, r], ps[:, AB[h], :], at_hi[:, r].bitcast(F32), ALU.subtract).then_inc(q["atl"], 1)

            def add_outputs(j):
                dve.wait_ge(q["exp"], j + 1)
                chain.link(nc.vector.reciprocal(rinv[:, j:j + 1], rsum[:, j:j + 1]))
                nc.vector.tensor_scalar(w2[:, j, :], w[:, j, :], rinv[:, j:j + 1], None, ALU.mult).then_inc(q["w2"], 1)
                dve.wait_ge(q["w2"], j + 1)
                for n, e in enumerate((0, 1, 4, 5)):
                    z = 4 * j + e // 2
                    if n % 2 == 0:
                        dve.wait_ge(q["zz"], z + 1)
                    src = x if e == 0 else out
                    nc.vector.scalar_tensor_tensor(out[:, j, :], ps[:, OB[z], (e % 2) * C:(e % 2 + 1) * C], w2[:, j, e:e + 1],
                                                   src[:, j, :], ALU.mult, ALU.add).then_inc(q["z"], 1)
                    dve.wait_ge(q["z"], 4 * j + n + 1)

            def other_outputs(j):
                add_scaled(nc.vector, dve, chain, j)

            work = {"s": row_max, "t": take_probs, "a": attended_low, "o": add_outputs, "O": other_outputs}
            for n in range(E + 2):
                masked(n)
                if n == 2:
                    routing_weights()
            for e in range(E):
                run(work, early[e])
                if E + e + 2 < 2 * E:
                    masked(E + e + 2)
            run(work, late + " O7")

        @block.gpsimd
        def _(pool):
            chain = Chain(pool, q["pchain"])
            for j in range(TILES - 1):
                add_scaled(nc.gpsimd, pool, chain, j)

        @block.scalar
        def _(act):
            for n in range(4):
                h, ct = divmod(n, 2)
                act.wait_ge(q["tr"], n + 1)
                nc.scalar.copy(m.xt_hi[:, ct, h * HALF:(h + 1) * HALF], ps[:, XB[n], :]).then_inc(q["hi"], 1)
            for h in range(2):
                act.wait_ge(q["lt"], h + 1)
                nc.scalar.copy(lg_t[:, h * HALF:(h + 1) * HALF], ps[0:E, LT[h], :]).then_inc(q["ltc"], 1)
            act.wait_ge(q["m"], 1)
            nc.scalar.activation(w, gated, ACT.Exp).then_inc(q["gexp"], 1)
            def projected(h):
                r = slice(h * HALF, (h + 1) * HALF)
                act.wait_ge(q["qkv"], E * (h + 1))
                if h:
                    act.wait_ge(q["vt"], 1)
                nc.scalar.activation(qt[:, r], ps[:, QB[0], :], ACT.Copy, scale=float(D) ** -0.5).then_inc(q["ev"], 1)
                nc.scalar.copy(kt[:, r], ps[:, QB[1], :]).then_inc(q["ev"], 1)
                nc.scalar.copy(vt, ps[:, QB[2], :]).then_inc(q["ev"], 1)

            def take_values(h):
                act.wait_ge(q["vt"], h + 1)
                nc.scalar.copy(vv[:, 4 * h:4 * h + 4, :], ps[:, VB[h], :].rearrange("p (t d) -> p t d", t=4)).then_inc(q["v"], 1)

            def exponentials(i):
                act.wait_ge(q["nm"], i + 1)
                if i >= 2:
                    act.wait_ge(q["ptc"], before[i - 1])
                nc.scalar.activation(pp[:, i % 2, 0:(i + 1) * P], scores_of(i)[:, 0:(i + 1) * P], ACT.Exp, bias=nmax[:, i:i + 1],
                                     accum_out=rsum[:, i:i + 1]).then_inc(q["exp"], 1)

            def attended_high(h):
                act.wait_ge(q["pv"], h + 1)
                nc.scalar.copy(at_hi[:, h * HALF:(h + 1) * HALF], ps[:, AB[h], :]).then_inc(q["ath"], 1)

            def scale_outputs(j):
                act.wait_ge(q["w2"], j + 1)
                if j >= 2:
                    act.wait_ge(q["res"], j - 1)
                for e in (2, 3, 6, 7):
                    z = 4 * j + e // 2
                    if e % 2 == 0:
                        act.wait_ge(q["zz"], z + 1)
                    nc.scalar.activation(scaled[:, j % 2, e // 4 * 2 + e % 2, :], ps[:, OB[z], (e % 2) * C:(e % 2 + 1) * C], ACT.Copy,
                                         scale=w2[:, j, e:e + 1]).then_inc(q["y"], 1)

            work = {"v": take_values, "s": exponentials, "a": attended_high, "o": scale_outputs}
            projected(0)
            for e in range(E):
                run(work, early[e])
            projected(1)
            run(work, late.replace("s4 v1", "v1 s4"))

        @block.tensor
        def _(pe):
            for n in range(4):
                h, ct = divmod(n, 2)
                pe.wait_ge(q["xln"], 4 * h + 4)
                transpose_rows(nc, m, pe, m.xn, h, ct, XB[n]).then_inc(q["tr"], 1)
            for h in range(2):
                pe.wait_ge(q["lo"], 2 * h + 2)
                for ct in range(CT):
                    r = slice(h * HALF, (h + 1) * HALF)
                    last = three_pass(nc, ps[0:E, LT[h], :], m.sn_hi[:, ct], m.sn_lo[:, ct], m.xt_hi[:, ct, r], m.xt_lo[:, ct, r],
                                      ct == 0, ct == CT - 1)
                last.then_inc(q["lt"], 1)
            for t in range(TILES):
                if t % 4 == 0:
                    pe.wait_ge(q["ltc"], t // 4 + 1)
                last = nc.tensor.transpose(ps[:, LG, t * E:(t + 1) * E], lg_t[:, t * P:(t + 1) * P], m.const[0:E, K_ID:K_ID + E])
            last.then_inc(q["lg"], 1)

            def mask_rows(n):
                h, e = divmod(n, E)
                if n >= 2:
                    pe.wait_ge(q["xm"], 2 * (n - 1))
                for t in range(4):
                    last = nc.tensor.matmul(ps[:, MB[n % 2], t * P:(t + 1) * P], m16[:, 4 * h + t, e:e + 1].to_broadcast([P, P]),
                                            m.ident16[:], start=True, stop=True)
                last.then_inc(q["mb"], 1)

            def project(n):
                h, e = divmod(n, E)
                pe.wait_ge(q["xm"], 2 * n + 2)
                if n == E:
                    pe.wait_ge(q["ev"], 3)
                for i in range(3):
                    for ct in range(CT):
                        last = three_pass(nc, ps[:, QB[i], :], m.w_hi[:, i, e * CT + ct], m.w_lo[:, i, e * CT + ct],
                                          xmh[:, n % XM, ct], xml[:, n % XM, ct], e == 0 and ct == 0, e == E - 1 and ct == CT - 1)
                last.then_inc(q["qkv"], 1)

            def values(h):
                pe.wait_ge(q["ev"], 3 * h + 3)
                for t in range(4):
                    last = nc.tensor.transpose(ps[:, VB[h], t * P:(t + 1) * P], vt[:, t * P:(t + 1) * P], m.const[:, K_ID:K_ID + P])
                last.then_inc(q["vt"], 1)

            def scores(i):
                pe.wait_ge(q["ev"], 6 if i >= 4 else 3)
                if i == 5:
                    pe.wait_ge(q["atl"], 1)
                if i >= 2:
                    pe.wait_ge(q["exp"], i - 1)
                n = (i + 1) * P
                for a in range(0, n, HALF):
                    z = min(n, a + HALF)
                    last = nc.tensor.matmul(ps[:, score_bank(i) + a // HALF, 0:z - a], qt[:, i * P:(i + 1) * P], kt[:, a:z],
                                            start=True, stop=True)
                last.then_inc(q["s"], 1)

            def turn_probs(j):
                pe.wait_ge(q["exp"], j + 1)
                if j == 0:
                    pe.wait_ge(q["v"], 1)
                if j == 4 and EARLY:
                    pe.wait_ge(q["z"], 4 * EARLY)
                    pe.wait_ge(q["y"], 4 * EARLY)
                for c, (k0, k1) in enumerate(chunks(j)):
                    n = before[j] + c
                    if n:
                        pe.wait_ge(q["pte"], n if n <= 4 else n - 1)
                    for k in range(k0, k1):
                        last = nc.tensor.transpose(ps[:, probs_bank(n), (k - k0) * P:(k - k0 + 1) * P],
                                                   pp[:, j % 2, k * P:(k + 1) * P], m.const[:, K_ID:K_ID + P])
                    last.then_inc(q["ptc"], 1)

            def attend(h):
                pe.wait_ge(q["pte"], before[4 * h + 4])
                pe.wait_ge(q["v"], h + 1)
                pe.wait_ge(q["exp"], 4 * h + 4)
                keys = 4 * h + 4
                for k in range(keys):
                    q0 = max(0, k - 4 * h) * P
                    last = nc.tensor.matmul(ps[:, AB[h], q0:HALF], vv[:, k, :], pt[h][:, k, q0:HALF], start=k == 0, stop=k == keys - 1)
                last.then_inc(q["pv"], 1)

            def outputs(j):
                pe.wait_ge(q["atl"], j // 4 + 1)
                if j == EARLY:
                    pe.wait_ge(q["v"], 2)
                for ep in range(4):
                    z = 4 * j + ep
                    if OB[z] in OB[:z]:
                        last_use = z - 1 - OB[:z][::-1].index(OB[z])
                        pe.wait_ge(q["z" if last_use % 2 == 0 else "y"], 2 * (last_use // 2 + 1))
                    r, c = slice(j * P, (j + 1) * P), slice(2 * ep * C, (2 * ep + 2) * C)
                    three_pass(nc, ps[:, OB[z], :], at_hi[:, r], at_lo[:, r], m.o_hi[:, c], m.o_lo[:, c], True, True).then_inc(q["zz"], 1)

            work = {"v": values, "s": scores, "t": turn_probs, "a": attend, "o": outputs}
            pe.wait_ge(q["m"], 1)
            mask_rows(0)
            for n in range(2 * E):
                if n + 1 < 2 * E:
                    mask_rows(n + 1)
                project(n)
                if n >= E:
                    run(work, early[n - E])
            run(work, late)


ATT_SEMS = ("chain pchain u ss rs tr hi lo lat latc pj qkv sqd rsq rsp qn khi hl va xb qkt qkc s e "
            "at att an tr2 hi2 lo2 o r used")


def attention(nc, m, q, local):
    HS = H + KVH
    HP = TILES // 2
    v = m.carve(("qkv", TILES * QKV, F32), ("rot", TILES * QK, F32), ("t", HP * QK, F32), ("qe", HP * H * 4 * HD, F16),
                ("ke", HP * KVH * 8 * HD, F16), ("qt", TILES * S, F16), ("kt", KVH * S, F16), ("va", TILES * KVH * 32, F32),
                ("sums", HP * HS, F32), ("guess", HP * HS, F32), ("norms", HP * HS, F32), ("early", 2 * HP * QK, F32))
    U = m.xa
    qkv = v["qkv"].rearrange("p (t n) -> p t n", t=TILES)
    rot = v["rot"].rearrange("p (t n) -> p t n", t=TILES)
    qn = v["t"][:, 0:HP * H * HD].rearrange("p (n d) -> p n d", d=HD)
    kn = v["t"][:, HP * H * HD:].rearrange("p (n d) -> p n d", d=HD)
    qe = v["qe"].rearrange("p (n s d) -> p n s d", s=4, d=HD)
    ke = v["ke"].rearrange("p (n z s d) -> p n z s d", z=2, s=4, d=HD)
    qt = v["qt"].rearrange("p (r n) -> p r n", r=H // 2)
    kt = v["kt"].rearrange("p (g n) -> p g n", g=KVH)
    va = v["va"].rearrange("p (t g d) -> p t g d", t=TILES, g=KVH)
    place = [("early", 0), ("early", 1), ("qkv", 0), ("qkv", 1), ("qkv", 2), ("rot", 0)]
    pr = [v[name][:, i * 2 * HALF:(i + 1) * 2 * HALF].rearrange("p (j n) -> p j n", j=2) for name, i in place]
    rot_t = v["early"][:, 0:HP * QK]
    qt_word = TILES * QKV + TILES * QK + HP * QK + HP * H * 2 * HD + HP * KVH * 4 * HD
    squares = [v["early"][:, HP * QK:2 * HP * QK], m.at_xt_lo[:].rearrange("p t n -> p (t n)")[:, 0:HP * QK]]
    lat_t = m.at("lat", qt_word, S)[0:LAT, :]
    row_junk = m.at("junk", qt_word, TILES * C).rearrange("p (t c) -> p t c", t=TILES)
    at = [m.at_xt_lo[:, i, HALF:] for i in range(2)]
    ms, ss, rs, guess8 = (m.small[:, i, :] for i in (6, 2, 3, 4))
    rc = m.rc[:].rearrange("p (t h) -> p t h", t=4)
    ps, ps16 = m.ps, m.ps[:].bitcast(F16)
    cos = m.const[:, K_COS + 128 * local:K_COS + 128 * local + 64].rearrange("p (t f) -> p t f", t=TILES)
    sin = m.const[:, K_COS + 128 * local + 64:K_COS + 128 * local + 128].rearrange("p (t f) -> p t f", t=TILES)

    def rotary(h):
        r, shape = slice(HP * h, HP * h + HP), [P, HP, HS, HD // 2]
        pair = qkv[:, r, 0:QK].rearrange("p t (h f z) -> p t h f z", h=HS, z=2)
        to = rot[:, r, :].rearrange("p t (h f z) -> p t h f z", h=HS, z=2)
        cb, sb_ = (x[:, r, :].unsqueeze(2).to_broadcast(shape) for x in (cos, sin))
        return pair[:, :, :, :, 0], pair[:, :, :, :, 1], to, cb, sb_

    wo = GW + LW + (C if local else 0)
    XB, JB, LB = [0, 1, 6, 7], [2, 3], [4, 5]
    QKB = [6, 4, 5, 7, 0, 1] + 6 * [7]
    PIECES = [("k", 0), ("q", 0), ("q", 1), ("k", 2), ("q", 2), ("q", 3), ("k", 4), ("k", 6), ("q", 4), ("q", 5), ("q", 6), ("q", 7)]

    def piece(j):
        kind, t = PIECES[j]
        if kind == "q":
            return qt[:, :, t * P:(t + 1) * P], ps16[:, QKB[j], :].rearrange("p (r n) -> p r n", n=P)
        return (kt[:, :, t * P:(t + 2) * P].rearrange("p g (t n) -> p t g n", t=2),
                ps16[:, QKB[j], :].rearrange("p (t g n) -> p t g n", t=2, n=P))

    SB, VB, AB = [0, 2], [4, 5], 6
    OB = [7, 7, 0, 1]

    steps, unit_end = [], []
    per = 1 if local else 2
    for h in range(2):
        for g in range(KVH):
            for k in range(4 * h + 4):
                a0, a1 = max(k * P, h * HALF), (h + 1) * HALF
                if local:
                    a1 = min(a1, k * P + SPAN)
                for a in range(per):
                    if a1 > a0:
                        steps.append((g, h, k, a, a0, a1 - a0, a0 - k * P))
            unit_end.append(len(steps))

    plan, pending = [], []
    side = [("w", 1)] + [("q", j) for j in range(6, 12)]
    start = 3
    for i, n in enumerate(range(0, len(steps) + LAG * per, per)):
        if unit_end[3] <= n < unit_end[3] + per:
            plan += side
            side = []
        if n < len(steps):
            plan.append(("s", n))
        if n >= LAG * per:
            done = n - LAG * per + per
            plan.append(("p", done - per))
            plan += [("t", u) for u in pending]
            if pending == [3]:
                side = [("x", 0), ("x", 1), ("o", 0), ("o", 1)]
            pending = [u for u, end in enumerate(unit_end) if end == done]
            plan += [("u", u) for u in pending]
        if i >= start and side:
            plan.append(side.pop(0))
    plan += [("t", u) for u in pending] + side

    def follow(work):
        for kind, i in plan:
            if kind in work:
                work[kind](i)

    with nc.Block() as block:
        @block.gpsimd
        def _(pool):
            chain = Chain(pool, q["pchain"])
            chain.link(nc.gpsimd.memset(va, 0.0))
            chain.link(nc.gpsimd.memset(va[:, :, :, HD:HD + 1], 1.0))
            for h in range(2):
                r = slice(HP * h, HP * h + HP)
                pool.wait_ge(q["qkv"], HP * h + HP)
                even, odd, to, cb, sb_ = rotary(h)
                p1, p2 = (m.xn[:, i, :].rearrange("p t c -> p (t c)")[:, 0:HP * QK // 2].rearrange("p (t h f) -> p t h f", t=HP, h=HS)
                          for i in (slice(0, 4), slice(4, 8)))
                if h:
                    pool.wait_ge(q["rsp"], h)
                chain.done(nc.gpsimd.tensor_tensor(p1, even, sb_, ALU.mult))
                chain.link(nc.gpsimd.tensor_tensor(p2, odd, cb, ALU.mult))
                nc.gpsimd.tensor_tensor(to[:, :, :, :, 1], p1, p2, ALU.add).then_inc(q["rsp"], 1)
                nc.gpsimd.tensor_copy(va[:, r, :, 0:HD], qkv[:, r, QK:].rearrange("p t (g d) -> p t g d", d=HD)).then_inc(q["va"], 1)
            if local:
                for h in range(2):
                    r = slice(HP * h, HP * h + HP)
                    nc.gpsimd.tensor_tensor(m.xb[:, r, :], m.xb[:, r, :], U[:, r, :], ALU.add).then_inc(q["xb"], 1)

        @block.vector
        def _(dve):
            chain = Chain(dve, q["chain"])
            if local:
                dve.wait_ge(q["ss"], TILES)
                chain.link(nc.vector.tensor_scalar(ms, ss, 1.0 / C, 1e-6, ALU.mult, ALU.add))
            else:
                layernorm(nc, m, dve, chain, m.xb, U, lambda h: None, lambda ins: ins.then_inc(q["u"], 1))
                normed_mean_square(nc, m, chain, ms)
                chain.link(nc.vector.tensor_scalar(ms, ms, 1e-6, None, ALU.add))
            rsqrt(nc, chain, rs, guess8, ms)
            dve.sem_inc(q["rs"], 1)
            for n in range(4):
                h, ct = divmod(n, 2)
                r = slice(h * HALF, (h + 1) * HALF)
                dve.wait_ge(q["hi"], n + 1)
                nc.vector.tensor_tensor(m.xt_lo[:, ct, r], ps[:, XB[n], :], m.xt_hi[:, ct, r].bitcast(F32),
                                        ALU.subtract).then_inc(q["lo"], 1)

            def rope(h):
                even, odd, to, cb, sb_ = rotary(h)
                t1, t2 = (rot_t[:, i * HP * QK // 2:(i + 1) * HP * QK // 2].rearrange("p (t h f) -> p t h f", t=HP, h=HS) for i in range(2))
                dve.wait_ge(q["qkv"], HP * h + HP)
                if h:
                    dve.wait_ge(q["rsq"], h)
                chain.done(nc.vector.tensor_tensor(t1, even, cb, ALU.mult))
                chain.link(nc.vector.tensor_tensor(t2, odd, sb_, ALU.mult))
                nc.vector.tensor_tensor(to[:, :, :, :, 0], t1, t2, ALU.subtract).then_inc(q["rsq"], 1)

            sums, guess, norms = (v[n_] for n_ in ("sums", "guess", "norms"))

            def head_sums(h):
                dve.wait_ge(q["sqd"], h + 1)
                chain.link(nc.vector.tensor_reduce(sums, squares[h].rearrange("p (n d) -> p n d", d=HD), AX.X, ALU.add))

            def head_norms(h):
                chain.link(nc.vector.tensor_scalar(sums, sums, 1.0 / HD, 1e-6, ALU.mult, ALU.add))
                rsqrt(nc, chain, norms, guess, sums)
                dve.wait_ge(q["rsq"], h + 1)
                dve.wait_ge(q["rsp"], h + 1)
                nv = norms.rearrange("p (t h) -> p t h", t=HP)
                for o, h0, hn in ((kn, H, KVH), (qn, 0, H)):
                    nc.vector.tensor_tensor(o.rearrange("p (t h) d -> p t h d", t=HP),
                                            rot[:, HP * h:HP * h + HP, h0 * HD:(h0 + hn) * HD].rearrange("p t (h d) -> p t h d", d=HD),
                                            nv[:, :, h0:h0 + hn].unsqueeze(3).to_broadcast([P, HP, hn, HD]), ALU.mult).then_inc(q["qn"], 1)

            def two_parts(h):
                dve.wait_ge(q["qn"], 2 * (h + 1))
                if h:
                    dve.wait_ge(q["qkt"], 6)
                    for z in range(2):
                        chain.done(nc.vector.tensor_copy(ke[:, :, z, 0:2, :], kn.unsqueeze(2).to_broadcast([P, HP * KVH, 2, HD])))
                else:
                    dve.wait_ge(q["khi"], 2)
                chain.link(nc.vector.tensor_copy(qe[:, :, 0::2, :], qn.unsqueeze(2).to_broadcast([P, HP * H, 2, HD])))
                for z in range(2):
                    nc.vector.tensor_tensor(ke[:, :, z, 2:4, :], kn.unsqueeze(2).to_broadcast([P, HP * KVH, 2, HD]),
                                            ke[:, :, z, 0:2, :], ALU.subtract).then_inc(q["hl"], 1)
                nc.vector.tensor_tensor(qe[:, :, 1::2, :], qn.unsqueeze(2).to_broadcast([P, HP * H, 2, HD]), qe[:, :, 0::2, :],
                                        ALU.subtract).then_inc(q["hl"], 1)

            def take_piece(j):
                dve.wait_ge(q["qkt"], j + 1)
                to, src = piece(j)
                nc.vector.tensor_copy(to, src).then_inc(q["qkc"], 1)

            rope(0)
            head_sums(0)
            head_norms(0)
            two_parts(0)
            rope(1)
            take_piece(2)
            take_piece(5)
            head_sums(1)
            head_norms(1)

            def unit_out(u):
                dve.wait_ge(q["used"], unit_end[u])
                if u >= 2:
                    dve.wait_ge(q["att"], u - 1)
                nc.vector.tensor_copy(at[u % 2], ps[:, VB[u % 2], :]).then_inc(q["at"], 1)

            def unit_norm(u):
                h, g = divmod(u, KVH)
                dve.wait_ge(q["att"], u + 1)
                a = ps[:, AB, :].rearrange("p (t h d) -> p t h d", t=4, h=4)
                chain.link(nc.vector.reciprocal(rc, a[:, :, :, HD]))
                nc.vector.tensor_tensor(m.xn[:, 4 * h:4 * h + 4, g * 64:(g + 1) * 64].rearrange("p t (h d) -> p t h d", d=HD),
                                        a[:, :, :, 0:HD], rc.unsqueeze(3).to_broadcast([P, 4, 4, HD]), ALU.mult).then_inc(q["an"], 1)

            def take_rows(n):
                dve.wait_ge(q["tr2"], n + 1)
                r = slice(0, HALF)
                nc.vector.tensor_copy(m.xt_hi[:, n, r], ps[:, OB[0], :]).then_inc(q["hi2"], 1)
                dve.wait_ge(q["hi2"], n + 1)
                nc.vector.tensor_tensor(m.xt_lo[:, n, r], ps[:, OB[0], :], m.xt_hi[:, n, r].bitcast(F32), ALU.subtract).then_inc(q["lo2"], 1)

            def add_outputs(j):
                dve.wait_ge(q["o"], j + 1)
                both = slice(2 * j, 2 * j + 2)
                if local:
                    dve.wait_ge(q["xb"], j // 2 + 1)
                to = m.xb if local else U
                nc.vector.tensor_tensor(to[:, both, :], to[:, both, :], ps[:, OB[j], :].rearrange("p (t c) -> p t c", t=2),
                                        ALU.add).then_inc(q["r"], 1)

            follow({"u": unit_out, "t": unit_norm, "w": two_parts, "q": take_piece, "x": take_rows, "o": add_outputs})
            for ct in range(2):
                dve.wait_ge(q["hi2"], ct + 3)
                nc.vector.tensor_tensor(m.xt_lo[:, ct, HALF:], ps[:, VB[ct], :], m.xt_hi[:, ct, HALF:].bitcast(F32),
                                        ALU.subtract).then_inc(q["lo2"], 1)
            for j in (2, 3):
                add_outputs(j)

        @block.scalar
        def _(act):
            def take_row_half(n):
                h, ct = divmod(n, 2)
                act.wait_ge(q["tr"], n + 1)
                nc.scalar.copy(m.xt_hi[:, ct, h * HALF:(h + 1) * HALF], ps[:, XB[n], :]).then_inc(q["hi"], 1)

            if local:
                for t in range(TILES):
                    nc.scalar.activation(row_junk[:, t, :], U[:, t, :], ACT.Square, accum_out=ss[:, t:t + 1]).then_inc(q["ss"], 1)
                    if t % 4 == 3:
                        take_row_half(t // 4)
                for n in range(2, 4):
                    take_row_half(n)
            else:
                for n in range(4):
                    take_row_half(n)
            act.wait_ge(q["rs"], 1)
            for h in range(2):
                if not local:
                    act.wait_ge(q["lat"], h + 1)
                    nc.scalar.copy(lat_t[:, h * HALF:(h + 1) * HALF], ps[0:LAT, LB[h], :]).then_inc(q["latc"], 1)
                for t in range(HP * h, HP * h + HP):
                    act.wait_ge(q["pj"], t + 1)
                    nc.scalar.activation(qkv[:, t, :], ps[:, JB[t % 2], 0:QKV], ACT.Copy, scale=rs[:, t:t + 1]).then_inc(q["qkv"], 1)
                act.wait_ge(q["qkv"], HP * h + HP)
                nc.scalar.activation(squares[h].rearrange("p (t n) -> p t n", t=HP), qkv[:, HP * h:HP * h + HP, 0:QK],
                                     ACT.Square).then_inc(q["sqd"], 1)
            act.wait_ge(q["qn"], 1)
            for z in range(2):
                nc.scalar.copy(ke[:, :, z, 0:2, :], kn.unsqueeze(2).to_broadcast([P, HP * KVH, 2, HD])).then_inc(q["khi"], 1)
            for j in (0, 1, 3, 4):
                act.wait_ge(q["qkt"], j + 1)
                to, src = piece(j)
                nc.scalar.copy(to, src).then_inc(q["qkc"], 1)
            act.wait_ge(q["va"], 2)
            act.wait_ge(q["rsq"], 2)

            def exponentials(n0):
                for n in range(n0, min(n0 + per, len(steps))):
                    w = steps[n][5]
                    act.wait_ge(q["s"], n + 1)
                    if n >= PR:
                        act.wait_ge(q["used"], n - PR + 1)
                    w_ = 2 * w if local else w
                    nc.scalar.activation(pr[n % PR][:, :, 0:w_], ps[:, SB[n % 2]:SB[n % 2] + 2, 0:w_], ACT.Exp,
                                         scale=float(HD) ** -0.5).then_inc(q["e"], 1)

            follow({"s": exponentials})
            for ct in range(2):
                act.wait_ge(q["tr2"], ct + 3)
                nc.scalar.copy(m.xt_hi[:, ct, HALF:], ps[:, VB[ct], :]).then_inc(q["hi2"], 1)

        @block.tensor
        def _(pe):
            for n in range(4):
                h, ct = divmod(n, 2)
                if not local:
                    pe.wait_ge(q["u"], 4 * h + 4)
                transpose_rows(nc, m, pe, U, h, ct, XB[n]).then_inc(q["tr"], 1)
            for h in range(2):
                pe.wait_ge(q["lo"], 2 * h + 2)
                if not local:
                    r = slice(h * HALF, (h + 1) * HALF)
                    for ct in range(CT):
                        last = three_pass(nc, ps[:, LB[h], :], m.a_hi[:, ct, 0:P], m.a_lo[:, ct, 0:P], m.xt_hi[:, ct, r],
                                          m.xt_lo[:, ct, r], ct == 0, ct == CT - 1)
                    last.then_inc(q["lat"], 1)
                for t in range(4 * h, 4 * h + 4):
                    r = slice(t * P, (t + 1) * P)
                    if t >= 2:
                        pe.wait_ge(q["qkv"], t - 1)
                    c0, n = (GW, QKV) if local else (LAT, H * HD)
                    for ct in range(CT):
                        last = three_pass(nc, ps[:, JB[t % 2], 0:n], m.xt_hi[:, ct, r], m.xt_lo[:, ct, r],
                                          m.a_hi[:, ct, c0:c0 + n], m.a_lo[:, ct, c0:c0 + n], ct == 0, ct == CT - 1)
                    if not local:
                        pe.wait_ge(q["latc"], h + 1)
                        last = nc.tensor.matmul(ps[:, JB[t % 2], n:QKV], lat_t[:, r], m.kv_up[:], start=True, stop=True)
                    last.then_inc(q["pj"], 1)

            def turn_piece(j):
                kind, t = PIECES[j]
                pe.wait_ge(q["hl"], 3 * (t // HP) + (2 if kind == "k" else 3))
                if j >= 6:
                    pe.wait_ge(q["qkc"], j)
                if kind == "q":
                    for i in range(H // 2):
                        n = (t % HP) * H + 2 * i
                        src = qe[:, n:n + 2].rearrange("p h s d -> p (h s d)")
                        last = nc.tensor.transpose(ps16[:, QKB[j], i * P:(i + 1) * P], src, m.ident16[:])
                else:
                    for i in range(2 * KVH):
                        src = ke[:, (t % HP) * KVH + i].rearrange("p z s d -> p (z s d)")
                        last = nc.tensor.transpose(ps16[:, QKB[j], i * P:(i + 1) * P], src, m.ident16[:])
                last.then_inc(q["qkt"], 1)

            for j in range(6):
                turn_piece(j)
            pe.wait_ge(q["va"], 1)

            def scores(n0):
                g, h, k, a, q0, w, d = steps[n0]
                pe.wait_ge(q["qkc"], 6 * (h + 1))
                keys = slice(k * P, (k + 1) * P)
                for n in range(n0, n0 + per):
                    a = n - n0
                    if n >= 2:
                        pe.wait_ge(q["e"], n - 1)
                    banks = (SB[n % 2], SB[n % 2] + 1)
                    for i in range(2):
                        rows = slice(64 * i, 64 * i + 64)
                        if local:
                            nc.tensor.matmul(ps[:, banks[i], 0:2 * w], m.ident16[:], m.win16[:, :, d:d + w], start=True, stop=False)
                            for j in range(2):
                                last = nc.tensor.matmul(ps[:, banks[i], j * w:(j + 1) * w], kt[rows, g, keys],
                                                        qt[rows, 2 * g + j, q0:q0 + w], start=False, stop=j == 1)
                        else:
                            c = 0
                            if d == 0:
                                c = P
                                nc.tensor.matmul(ps[:, banks[i], 0:P], m.ident16[:], m.tri16[:], start=True, stop=False)
                                last = nc.tensor.matmul(ps[:, banks[i], 0:P], kt[rows, g, keys], qt[rows, 2 * g + a, q0:q0 + P],
                                                        start=False, stop=True)
                            if c < w:
                                last = nc.tensor.matmul(ps[:, banks[i], c:w], kt[rows, g, keys], qt[rows, 2 * g + a, q0 + c:q0 + w],
                                                        start=True, stop=True)
                    last.then_inc(q["s"], 1)

            def products(n0):
                g, h, k, a, q0, w, d = steps[n0]
                u = h * KVH + g
                first = n0 == (unit_end[u - 1] if u else 0)
                if first and h and g == 0:
                    pe.wait_ge(q["va"], 2)
                if first and u >= 2:
                    pe.wait_ge(q["at"], u - 1)
                if first and local:
                    nc.tensor.matmul(ps[:, VB[u % 2], :], m.zeros16[:], m.zeros16[:].unsqueeze(1).to_broadcast([P, 4, P]),
                                     start=True, stop=True)
                pe.wait_ge(q["e"], n0 + per)
                for hd in range(4):
                    pair, i = divmod(hd, 2)
                    o = ps[32 * hd:32 * hd + 32, VB[u % 2], q0 - h * HALF:q0 - h * HALF + w]
                    if local:
                        last = nc.tensor.matmul(o, va[:, k, g, :], pr[n0 % PR][:, i, pair * w:(pair + 1) * w],
                                                start=False, stop=True, skip_group_check=True)
                    else:
                        last = nc.tensor.matmul(o, va[:, k, g, :], pr[(n0 + pair) % PR][:, i, 0:w], start=k == 0, stop=k == 4 * h + 3)
                last.then_inc(q["used"], per)

            def turn(u):
                pe.wait_ge(q["at"], u + 1)
                if u:
                    pe.wait_ge(q["an"], u)
                for t in range(4):
                    last = nc.tensor.transpose(ps[:, AB, t * P:(t + 1) * P], at[u % 2][:, t * P:(t + 1) * P], m.const[:, K_ID:K_ID + P])
                last.then_inc(q["att"], 1)

            def turn_rows(ct):
                pe.wait_ge(q["an"], KVH)
                if ct:
                    pe.wait_ge(q["lo2"], ct)
                transpose_rows(nc, m, pe, m.xn, 0, ct, OB[0]).then_inc(q["tr2"], 1)

            def outputs(j):
                if j < 2:
                    pe.wait_ge(q["lo2"], 2)
                if j == 1:
                    pe.wait_ge(q["r"], 1)
                for t in (2 * j, 2 * j + 1):
                    r = slice(t * P, (t + 1) * P)
                    for ct in range(CT):
                        last = three_pass(nc, ps[:, OB[j], (t % 2) * C:(t % 2 + 1) * C], m.xt_hi[:, ct, r], m.xt_lo[:, ct, r],
                                          m.a_hi[:, ct, wo:wo + C], m.a_lo[:, ct, wo:wo + C], ct == 0, ct == CT - 1)
                last.then_inc(q["o"], 1)

            follow({"s": scores, "p": products, "t": turn, "q": turn_piece, "x": turn_rows, "o": outputs})
            pe.wait_ge(q["an"], 2 * KVH)
            for ct in range(2):
                transpose_rows(nc, m, pe, m.xn, 1, ct, VB[ct]).then_inc(q["tr2"], 1)
            pe.wait_ge(q["lo2"], 4)
            for j in (2, 3):
                outputs(j)


def build(nc, ins, out):
    ctx = ExitStack()
    with ctx:
        m = Mem(nc, ctx)
        qs = semaphores(nc, ctx, "setup", SETUP_SEMS)
        qf, qa = semaphores(nc, ctx, "ffn", FFN_SEMS), semaphores(nc, ctx, "att", ATT_SEMS)
        x = ins["L0_attn_hidden"]
        setup(nc, m, qs, ins)
        with nc.Fori(0, B) as b:
            ffn(nc, m, qf, b, x, out, True)
            clear(nc, qf)
            for local in (False, True):
                attention(nc, m, qa, local)
                clear(nc, qa)
            ffn(nc, m, qf, b, x, out, False)
            clear(nc, qf)


_INS = ["L0_attn_hidden", "L0_attn_norm1_w", "L0_attn_norm2_w", "L0_attn_g_wq", "L0_attn_g_kv_down", "L0_attn_g_k_up",
        "L0_attn_g_v_up", "L0_attn_g_wo", "L0_attn_l_wq", "L0_attn_l_wk", "L0_attn_l_wv", "L0_attn_l_wo", "L0_ffn_sim_matrix",
        "L0_ffn_gates", "L0_ffn_q_proj", "L0_ffn_k_proj", "L0_ffn_v_proj", "L0_ffn_o_proj"]


def constants():
    import numpy as np
    c = np.zeros((P, K_ALL), np.float32)
    i, j = np.arange(P)[:, None], np.arange(P)[None, :]
    c[:, K_ID:K_ID + P] = i == j
    c[:, K_NEG:K_NEG + P] = np.where(j > i, -1e30, 0.0)
    c[:, K_TRI:K_TRI + P] = j >= i
    d = np.arange(SPAN)[None, :] - i
    c[:, K_WIN:K_WIN + SPAN] = (d >= 0) & (d < WIN)
    e = np.arange(E)
    c[:, K_TRI8:K_TRI8 + E * E] = (e[None, :] < e[:, None]).astype(np.float32).reshape(1, -1)
    for n, base in enumerate((1000000.0, 10000.0)):
        inv = (np.float32(1.0) / np.float32(base) ** (np.arange(0, HD, 2, dtype=np.float32) / np.float32(HD))).astype(np.float32)
        f = (np.arange(S, dtype=np.float32)[:, None] * inv[None, :]).reshape(TILES, P, HD // 2).transpose(1, 0, 2).reshape(P, 64)
        c[:, K_COS + 128 * n:K_COS + 128 * n + 64] = np.cos(f)
        c[:, K_COS + 128 * n + 64:K_COS + 128 * n + 128] = np.sin(f)
    return c


def kernel(**inputs):
    import numpy as np
    import concourse.bacc as bacc
    from concourse.bass_utils import run_bass_kernel_spmd

    nc = bacc.Bacc("TRN2", target_bir_lowering=False, num_devices=1)
    arrays, ins = {}, {}
    for name in _INS:
        a = np.ascontiguousarray(inputs[name])
        arrays[f"in_{name}"] = a
        ins[name] = nc.dram_tensor(f"in_{name}", a.shape, mybir.dt.from_np(a.dtype), kind="ExternalInput").ap()
    arrays["in_const"] = constants()
    ins["const"] = nc.dram_tensor("in_const", (P, K_ALL), F32, kind="ExternalInput").ap()
    out = nc.dram_tensor("out_dram", (B, S, C), F32, kind="ExternalOutput").ap()
    build(nc, ins, out)
    r = run_bass_kernel_spmd(nc, [arrays], core_ids=[0])
    return r.results[0]["out_dram"]
```

```python
import concourse.bass as bass
from concourse import mybir
from contextlib import ExitStack

P = 128
B, S, C = 4, 1024, 256
TILES = S // P
CT = C // P
HALF = 512
E, D = 8, 128
H, KVH, HD = 16, 4, 16
LAT = 64
WIN = 64
QK = (H + KVH) * HD
QKV = QK + KVH * HD
GW = LAT + H * HD
LW = QKV
AW = GW + LW + 2 * C
SPAN = P + WIN
XM = 4
PR = 6
STORE = 2
LAG = 2
MASKED = -30000.0

K_ID, K_NEG, K_WIN, K_TRI8, K_COS = 0, 128, 256, 256 + SPAN, 256 + SPAN + 64
K_TRI = K_COS + 4 * 64
K_ALL = K_TRI + 128

F32, F16, F32R, I32 = mybir.dt.float32, mybir.dt.float16, mybir.dt.float32r, mybir.dt.int32
ALU, ACT, AX = mybir.AluOpType, mybir.ActivationFunctionType, mybir.AxisListType


class Mem:

    def __init__(self, nc, ctx):
        def sb(name, shape, dt=F32):
            return ctx.enter_context(nc.sbuf_tensor(name, shape, dt))
        self.const = sb("const", [P, K_ALL])
        self.ident16 = sb("ident16", [P, P], F16)
        self.zeros16 = sb("zeros16", [P, P], F16)
        self.win16 = sb("win16", [P, 2, SPAN], F16)
        self.tri16 = sb("tri16", [P, P], F16)
        self.w_hi = sb("w_hi", [P, 3, E * CT, D], F32R)
        self.w_lo = sb("w_lo", [P, 3, E * CT, D], F32R)
        self.o_hi = sb("o_hi", [P, E * C], F32R)
        self.o_lo = sb("o_lo", [P, E * C], F32R)
        self.a_hi = sb("a_hi", [P, CT, AW], F32R)
        self.a_lo = sb("a_lo", [P, CT, AW], F32R)
        self.kv_up = sb("kv_up", [LAT, 2 * KVH * HD])
        self.sn_hi = sb("sn_hi", [P, CT, E], F32R)
        self.sn_lo = sb("sn_lo", [P, CT, E], F32R)
        self.sig = sb("sig", [P, E])
        self.norm_w = sb("norm_w", [P, 2, CT])
        self.xa = sb("xa", [P, TILES, C])
        self.xb = sb("xb", [P, TILES, C])
        self.xn = sb("xn", [P, TILES, C])
        self.xt_hi = sb("xt_hi", [P, CT, S], F32R)
        lo_base = nc.sbuf_base
        self.xt_lo = sb("xt_lo", [P, CT, S], F32R)
        self.stats = sb("stats", [P, TILES, 6])
        self.mv = sb("mv", [P, TILES, 2])
        self.small = sb("small", [P, 8, TILES])
        self.rc = sb("rc", [P, 16])
        self.arena_bytes = 78 * 1024
        self.nc, self.base, self.views = nc, nc.sbuf_base, 0
        sb("arena", [P, self.arena_bytes // 4])
        self.at_xt_lo = nc.alloc_sbuf_tensor_at("at_xt_lo", [P, CT, S], F32, offset=lo_base, align_bytes=4)
        self.ps = ctx.enter_context(nc.psum_tensor("ps", [P, 8, HALF], F32))

    def at(self, name, word, n, dt=F32):
        words = n // 2 if dt == F16 else n
        assert (word + words) * 4 <= self.arena_bytes, (name, word + words)
        self.views += 1
        return self.nc.alloc_sbuf_tensor_at(f"{name}_{self.views}", [P, n], dt, offset=self.base + 4 * word, align_bytes=4)[:]

    def carve(self, *parts):
        word, views = 0, {}
        for name, n, dt in parts:
            views[name] = self.at(name, word, n, dt)
            word += n // 2 if dt == F16 else n
        return views


class Chain:

    def __init__(self, eng, sem):
        self.eng, self.sem, self.n = eng, sem, 0

    def done(self, ins):
        self.n += 1
        ins.then_inc(self.sem, 1)

    def wait(self):
        self.eng.wait_ge(self.sem, self.n)

    def link(self, ins):
        self.done(ins)
        self.wait()


def semaphores(nc, ctx, stage, names):
    return {name: ctx.enter_context(nc.semaphore(f"{stage}_{name}")) for name in names.split()}


def rsqrt(nc, chain, out, t, x):
    chain.link(nc.vector.tensor_scalar(t.bitcast(I32), x.bitcast(I32), 1, None, ALU.logical_shift_right))
    chain.link(nc.vector.tensor_scalar(out.bitcast(I32), t.bitcast(I32), -1.0, float(0x5F3759DF), ALU.mult, ALU.add))
    for _ in range(3):
        chain.link(nc.vector.scalar_tensor_tensor(t, out, -0.5, out, ALU.mult, ALU.mult))
        chain.link(nc.vector.tensor_tensor(t, t, x, ALU.mult))
        last = nc.vector.scalar_tensor_tensor(out, t, 1.5, out, ALU.add, ALU.mult)
        chain.link(last)


SETUP_SEMS = "x const w0 w1 w2 oo aw misc cast stage hi chain pchain pre sq exp"


def setup(nc, m, q, stored, ins):
    v = m.carve(("wst", 3 * E * CT * D, F32), ("ost", E * C, F32), ("ast", CT * AW, F32),
                ("sim", CT * E, F32), ("sq", CT * E, F32), ("ones", P, F32), ("gt", E, F32), ("rn", E, F32), ("rt", E, F32))
    wst = v["wst"].rearrange("p (w k d) -> p w k d", w=3, d=D)
    ast = v["ast"].rearrange("p (t n) -> p t n", t=CT)
    sim = v["sim"].rearrange("p (t e) -> p t e", t=CT)
    sq = v["sq"].rearrange("p (t e) -> p t e", t=CT)
    ones, gt, rn, rt = v["ones"], v["gt"], v["rn"], v["rt"]
    norm_ps = m.ps[:, 0, 0:E]

    with nc.Block() as block:
        @block.sync
        def _(sp):
            sp.dma_start(m.const[:], ins["const"]).then_inc(q["const"], 16)
            load_rows(sp, m, q["x"], ins["L0_attn_hidden"], 0)
            sp.dma_start(sim, ins["L0_ffn_sim_matrix"].rearrange("(t p) e -> p t e", p=P)).then_inc(q["misc"], 16)
            sp.dma_start(m.norm_w[:, 0, :], ins["L0_attn_norm1_w"].rearrange("(t p) -> p t", p=P),
                         allow_slow_non_contiguous=True).then_inc(q["misc"], 16)
            sp.dma_start(m.norm_w[:, 1, :], ins["L0_attn_norm2_w"].rearrange("(t p) -> p t", p=P),
                         allow_slow_non_contiguous=True).then_inc(q["misc"], 16)
            sp.dma_start(gt, ins["L0_ffn_gates"].partition_broadcast(P)).then_inc(q["misc"], 16)
            for i, n in enumerate(("q", "k", "v")):
                sp.dma_start(wst[:, i], ins[f"L0_ffn_{n}_proj"].rearrange("e (t p) d -> p (e t) d", p=P)).then_inc(q[f"w{i}"], 16)
            sp.dma_start(v["ost"].rearrange("p (e c) -> p e c", e=E),
                         ins["L0_ffn_o_proj"].rearrange("e d c -> d e c")).then_inc(q["oo"], 16)
            sp.sem_inc(stored, 16 * TILES // STORE)
            sp.wait_ge(q["x"], 32)

        @block.gpsimd
        def _(pool):
            chain = Chain(pool, q["pchain"])
            chain.done(nc.gpsimd.memset(m.zeros16[:], 0.0))
            nc.gpsimd.memset(ones, 1.0).then_inc(q["pre"], 1)
            pool.wait_ge(q["hi"], 4)
            nc.gpsimd.tensor_tensor(m.o_lo[:], v["ost"], m.o_hi[:].bitcast(F32), ALU.subtract)

        @block.tensor
        def _(pe):
            pe.wait_ge(q["pre"], 1)
            pe.wait_ge(q["sq"], 1)
            for t in range(CT):
                ins_ = nc.tensor.matmul(norm_ps, ones, sq[:, t], start=t == 0, stop=t == CT - 1)
            ins_.then_inc(q["stage"], 1)

        @block.scalar
        def _(act):
            at = 0
            for name, n in (("L0_attn_g_kv_down", LAT), ("L0_attn_g_wq", C), ("L0_attn_l_wq", C), ("L0_attn_l_wk", KVH * HD),
                            ("L0_attn_l_wv", KVH * HD), ("L0_attn_g_wo", C), ("L0_attn_l_wo", C)):
                act.dma_start(ast[:, :, at:at + n], ins[name].rearrange("(t p) n -> p t n", p=P)).then_inc(q["aw"], 16)
                at += n
            act.dma_start(m.kv_up[:, 0:KVH * HD], ins["L0_attn_g_k_up"]).then_inc(q["aw"], 16)
            act.dma_start(m.kv_up[:, KVH * HD:], ins["L0_attn_g_v_up"]).then_inc(q["aw"], 16)
            act.wait_ge(q["misc"], 64)
            nc.scalar.activation(gt, gt, ACT.Exp, scale=-1.0).then_inc(q["exp"], 1)
            for i in range(3):
                act.wait_ge(q[f"w{i}"], 16)
                nc.scalar.copy(m.w_hi[:, i], wst[:, i]).then_inc(q["hi"], 1)
            act.wait_ge(q["oo"], 16)
            nc.scalar.copy(m.o_hi[:], v["ost"]).then_inc(q["hi"], 1)
            act.wait_ge(q["cast"], 4)
            nc.scalar.copy(m.a_hi[:], ast).then_inc(q["hi"], 1)

        @block.vector
        def _(dve):
            chain = Chain(dve, q["chain"])
            dve.wait_ge(q["misc"], 64)
            nc.vector.tensor_tensor(sq, sim, sim, ALU.mult).then_inc(q["sq"], 1)
            dve.wait_ge(q["const"], 16)
            nc.vector.tensor_copy(m.ident16[:], m.const[:, K_ID:K_ID + P])
            for j in range(2):
                nc.vector.tensor_scalar(m.win16[:, j, :], m.const[:, K_WIN:K_WIN + SPAN], -MASKED, MASKED, ALU.mult, ALU.add)
            nc.vector.tensor_scalar(m.tri16[:], m.const[:, K_TRI:K_TRI + P], -MASKED, MASKED, ALU.mult, ALU.add)
            dve.wait_ge(q["exp"], 1)
            chain.link(nc.vector.tensor_scalar(gt, gt, 1.0, None, ALU.add))
            chain.link(nc.vector.reciprocal(m.sig[:], gt))
            dve.wait_ge(q["stage"], 1)
            chain.link(nc.vector.tensor_scalar(gt, norm_ps, 1e-24, None, ALU.max))
            rsqrt(nc, chain, rn, rt, gt)
            chain.link(nc.vector.tensor_tensor(sim, sim, rn.unsqueeze(1).to_broadcast([P, CT, E]), ALU.mult))
            chain.link(nc.vector.tensor_copy(m.sn_hi[:], sim))
            chain.done(nc.vector.tensor_tensor(m.sn_lo[:], sim, m.sn_hi[:].bitcast(F32), ALU.subtract))
            dve.wait_ge(q["x"], 32)
            row_statistics(nc, m, chain, m.xa, range(TILES))
            for i in range(2):
                dve.wait_ge(q["hi"], i + 1)
                nc.vector.tensor_tensor(m.w_lo[:, i], wst[:, i], m.w_hi[:, i].bitcast(F32), ALU.subtract)
            dve.wait_ge(q["aw"], 16 * 9)
            for t in range(CT):
                for i, (a, n) in enumerate(((0, GW), (GW, LW))):
                    nc.vector.tensor_scalar(ast[:, t, a:a + n], ast[:, t, a:a + n], m.norm_w[:, i, t:t + 1], None,
                                            ALU.mult).then_inc(q["cast"], 1)
            dve.wait_ge(q["hi"], 3)
            nc.vector.tensor_tensor(m.w_lo[:, 2], wst[:, 2], m.w_hi[:, 2].bitcast(F32), ALU.subtract)
            dve.wait_ge(q["hi"], 5)
            nc.vector.tensor_tensor(m.a_lo[:], ast, m.a_hi[:].bitcast(F32), ALU.subtract)


def clear(nc, q):
    ids = [s.num for s in q.values()]
    assert max(ids) - min(ids) == len(ids) - 1
    nc.gpsimd.sem_clear(range(min(ids), max(ids) + 1))
    nc.all_engine_barrier()


FFN_SEMS = ("x chain xln tr hi lo lt ltc lg m gexp mb xm qkv ev vt v s nm exp ptc pte pv ath atl "
            "zz z w2 y pchain res last_res")


def row_statistics(nc, m, chain, x, tiles):
    for t in tiles:
        chain.done(nc.vector.bn_stats(m.stats[:, t, :], x[:, t, :]))
    chain.wait()
    for t in tiles:
        chain.done(nc.vector.bn_aggr(m.mv[:, t, :], m.stats[:, t, :]))


def layernorm(nc, m, chain, x, out, done):
    var, rstd, guess = (m.small[:, i, :] for i in (0, 1, 4))
    chain.link(nc.vector.tensor_scalar(var, m.mv[:, :, 1], 1e-5, None, ALU.add))
    rsqrt(nc, chain, rstd, guess, var)
    for t in range(TILES):
        done(nc.vector.tensor_scalar(out[:, t, :], x[:, t, :], m.mv[:, t, 0:1], rstd[:, t:t + 1],
                                     ALU.subtract, ALU.mult))


def normed_mean_square(nc, m, chain, out):
    rstd = m.small[:, 1, :]
    chain.link(nc.vector.tensor_tensor(out, m.mv[:, :, 1], rstd, ALU.mult))
    chain.link(nc.vector.tensor_tensor(out, out, rstd, ALU.mult))


def transpose_rows(nc, m, pe, src, h, ct, bank):
    for t in range(4):
        ins = nc.tensor.transpose(m.ps[:, bank, t * P:t * P + P], src[:, 4 * h + t, ct * P:ct * P + P],
                                  m.const[:, K_ID:K_ID + P])
    return ins


def three_pass(nc, out, w_hi, w_lo, x_hi, x_lo, first, last):
    nc.tensor.matmul(out, w_hi, x_hi, start=first, stop=False)
    nc.tensor.matmul(out, w_lo, x_hi, start=False, stop=False)
    return nc.tensor.matmul(out, w_hi, x_lo, start=False, stop=last)


def load_rows(sp, m, sem, x_dram, b):
    for h in range(2):
        sp.dma_start(m.xa[:, 4 * h:4 * h + 4, :],
                     x_dram[bass.ds(b, 1), h * HALF:(h + 1) * HALF, :].rearrange("b (t p) c -> p (b t) c", p=P)).then_inc(sem, 16)


def ffn(nc, m, q, stored, b, x_dram, out_dram, first):
    x, out = (m.xa, m.xb) if first else (m.xb, m.xb)
    v = m.carve(("xmh", XM * CT * HALF, F32R), ("xml", XM * CT * HALF, F32R), ("qt", S, F32), ("kt", S, F32),
                ("vt", HALF, F32), ("v", TILES * D, F32), ("p", 2 * S, F32), ("at_hi", S, F32R), ("at_lo", S, F32R),
                ("m16", TILES * E, F16), ("lg", TILES * E, F32), ("gated", TILES * E, F32), ("mask", TILES * E, F32),
                ("w", TILES * E, F32), ("w2", TILES * E, F32), ("cnt", TILES, F32), ("rsum", TILES, F32),
                ("nmax", TILES, F32), ("rinv", TILES, F32), ("g", TILES * E * E, F32),
                ("pt0", 4 * HALF, F32))
    xmh = v["xmh"].rearrange("p (r t n) -> p r t n", r=XM, t=CT)
    xml = v["xml"].rearrange("p (r t n) -> p r t n", r=XM, t=CT)
    pt = [v["pt0"].rearrange("p (k n) -> p k n", n=HALF), m.at("pt1", 0, TILES * HALF).rearrange("p (k n) -> p k n", n=HALF)]
    vv = v["v"].rearrange("p (t d) -> p t d", t=TILES)
    pp = v["p"].rearrange("p (r n) -> p r n", r=2)
    te = lambda n: v[n].rearrange("p (t e) -> p t e", t=TILES)
    m16, lg, gated, mask, w, w2 = (te(n) for n in ("m16", "lg", "gated", "mask", "w", "w2"))
    qt, kt, vt, at_hi, at_lo, cnt, rsum, nmax, rinv = (v[n] for n in
        ("qt", "kt", "vt", "at_hi", "at_lo", "cnt", "rsum", "nmax", "rinv"))
    lg_t = v["p"][0:E, 0:S]
    ps = m.ps
    ss, rn = m.small[:, 2, :], m.small[:, 3, :]
    XB = [0, 1, 4, 5]
    LT, LG = [6, 7], [2, 1]
    MB = [2, 3]
    QB = [4, 5, 6]
    VB = [0, 3]
    AB = [7, 4]
    score_bank = lambda i: [7, 1][i % 2] if i < 4 else [4, 6][i % 2]
    probs_bank = lambda n: 0 if n < 4 else n % 2
    OB = [2, 3] * 8 + [2, 3, 5, 6] * 4
    scaled = m.xn[:].rearrange("p (r e) c -> p r e c", r=2)

    def chunks(i):
        return [(k, min(k + 4, i + 1)) for k in range(0, i + 1, 4)]
    before = [sum(len(chunks(j)) for j in range(i)) for i in range(TILES + 1)]

    def scores_of(i):
        bank = score_bank(i)
        return (ps[:, bank:bank + 2, :] if i >= 4 else ps[:, bank:bank + 1, :]).rearrange("p b n -> p (b n)")

    early = {0: "v0", 1: "s0 s1", 2: "t0 s2", 3: "t1 s3", 4: "t2", 5: "t3 a0", 6: "", 7: ""}
    late = "s4 v1 s5 o0 t4 o1 s6 t5 s7 t6 o2 t7 a1 o3 o4 o5 o6 o7"

    def run(work, names):
        for name in names.split():
            if name[0] in work:
                work[name[0]](int(name[1]))

    def add_scaled(engine, eng, chain, j):
        part = scaled[:, j % 2]
        eng.wait_ge(q["y"], 4 * j + 4)
        chain.link(engine.tensor_tensor(part[:, 0:2, :], part[:, 0:2, :], part[:, 2:4, :], ALU.add))
        chain.link(engine.tensor_tensor(part[:, 0, :], part[:, 0, :], part[:, 1, :], ALU.add))
        eng.wait_ge(q["z"], 4 * j + 4)
        engine.tensor_tensor(out[:, j, :], out[:, j, :], part[:, 0, :], ALU.add).then_inc(q["last_res" if j == TILES - 1 else "res"], 1)

    with nc.Block() as block:
        @block.sync
        def _(sp):
            if not first:
                load_rows(sp, m, q["x"], x_dram, (b + 1) % B)
                for i in range(0, TILES, STORE):
                    if i + STORE < TILES:
                        sp.wait_ge(q["res"], i + STORE)
                    else:
                        sp.wait_ge(q["res"], TILES - 1)
                        sp.wait_ge(q["last_res"], 1)
                    sp.dma_start(out_dram[bass.ds(b, 1), i * P:(i + STORE) * P, :].rearrange("b (t p) c -> p (b t) c", p=P),
                                 out[:, i:i + STORE, :]).then_inc(stored, 16)
                sp.wait_ge(q["x"], 32)

        @block.vector
        def _(dve):
            chain = Chain(dve, q["chain"])
            layernorm(nc, m, chain, x, m.xn, lambda ins: ins.then_inc(q["xln"], 1))
            normed_mean_square(nc, m, chain, ss)
            chain.link(nc.vector.tensor_scalar(ss, ss, float(C), 1e-24, ALU.mult, ALU.max))
            rsqrt(nc, chain, rn, m.small[:, 4, :], ss)
            for n in range(4):
                h, ct = divmod(n, 2)
                r = slice(h * HALF, (h + 1) * HALF)
                dve.wait_ge(q["hi"], n + 1)
                nc.vector.tensor_tensor(m.xt_lo[:, ct, r], ps[:, XB[n], :], m.xt_hi[:, ct, r].bitcast(F32),
                                        ALU.subtract).then_inc(q["lo"], 1)
            full, cube = [P, 4, E], [P, 4, E, E]
            def route(h):
                r = slice(4 * h, 4 * h + 4)
                lgh, gh, mh, wh, ch, nh = lg[:, r], gated[:, r], mask[:, r], w2[:, r], cnt[:, r], nmax[:, r]
                dve.wait_ge(q["lg"], h + 1)
                chain.link(nc.vector.tensor_tensor(lgh, ps[:, LG[h], 0:4 * E].rearrange("p (t e) -> p t e", t=4),
                                                   rn[:, r].unsqueeze(2).to_broadcast(full), ALU.mult))
                chain.link(nc.vector.tensor_tensor(lgh, lgh, m.sig[:].unsqueeze(1).to_broadcast(full), ALU.subtract))
                chain.done(nc.vector.tensor_scalar(gh, lgh, 0.0, None, ALU.max))
                chain.done(nc.vector.tensor_scalar(mh, lgh, 0.0, None, ALU.is_gt))
                g = v["g"].rearrange("p (t e j) -> p t e j", t=TILES, e=E)[:, 0:4]
                eq = v["g"].rearrange("p (t e j) -> p t e j", t=TILES, e=E)[:, 4:8]
                le, lj = lgh.unsqueeze(3).to_broadcast(cube), lgh.unsqueeze(2).to_broadcast(cube)
                chain.done(nc.vector.tensor_tensor(g, lj, le, ALU.is_gt))
                chain.link(nc.vector.tensor_tensor(eq, lj, le, ALU.is_equal))
                lower = m.const[:, K_TRI8:K_TRI8 + 64].rearrange("p (e j) -> p e j", e=E).unsqueeze(1).to_broadcast(cube)
                chain.link(nc.vector.tensor_tensor(eq, eq, lower, ALU.mult))
                chain.link(nc.vector.tensor_tensor(g, g, eq, ALU.add))
                chain.done(nc.vector.tensor_reduce(wh, g, AX.X, ALU.add))
                chain.done(nc.vector.tensor_reduce(ch, mh, AX.X, ALU.add))
                chain.link(nc.vector.tensor_reduce(nh, gh, AX.X, ALU.max))
                chain.done(nc.vector.tensor_scalar(wh, wh, 2.0, None, ALU.is_lt))
                chain.done(nc.vector.tensor_tensor(gh, gh, nh.unsqueeze(2).to_broadcast(full), ALU.subtract))
                chain.link(nc.vector.tensor_scalar(ch, ch, 0.0, None, ALU.is_equal))
                chain.link(nc.vector.tensor_tensor(wh, wh, ch.unsqueeze(2).to_broadcast(full), ALU.mult))
                chain.link(nc.vector.tensor_tensor(mh, mh, wh, ALU.max))
                nc.vector.tensor_copy(m16[:, r], mh).then_inc(q["m"], 1)

            def routing_weights():
                dve.wait_ge(q["gexp"], 1)
                chain.link(nc.vector.tensor_tensor(w, w, mask, ALU.mult))
                chain.link(nc.vector.tensor_reduce(cnt, w, AX.X, ALU.add))
                chain.link(nc.vector.reciprocal(cnt, cnt))
                chain.link(nc.vector.tensor_scalar(cnt, cnt, 0.5, None, ALU.mult))
                chain.link(nc.vector.tensor_tensor(w, w, cnt.unsqueeze(2).to_broadcast([P, TILES, E]), ALU.mult))

            def masked(n):
                h, e = divmod(n, E)
                r = slice(h * HALF, (h + 1) * HALF)
                dve.wait_ge(q["mb"], n + 1)
                if n >= XM:
                    dve.wait_ge(q["qkv"], n - XM + 1)
                mb = ps[:, MB[n % 2], :].unsqueeze(1).to_broadcast([P, CT, HALF])
                for o, i in ((xmh, m.xt_hi), (xml, m.xt_lo)):
                    nc.vector.tensor_tensor(o[:, n % XM], i[:, :, r].bitcast(F32), mb, ALU.mult).then_inc(q["xm"], 1)

            def row_max(i):
                dve.wait_ge(q["s"], i + 1)
                sc = scores_of(i)
                dg = sc[:, i * P:(i + 1) * P]
                chain.link(nc.vector.tensor_tensor(dg, dg, m.const[:, K_NEG:K_NEG + P], ALU.add))
                nc.vector.tensor_reduce(nmax[:, i:i + 1], sc[:, 0:(i + 1) * P], AX.X, ALU.max, negate=True).then_inc(q["nm"], 1)

            def take_probs(j):
                for c, (k0, k1) in enumerate(chunks(j)):
                    n = before[j] + c
                    dve.wait_ge(q["ptc"], n + 1)
                    nc.vector.tensor_copy(pt[j // 4][:, k0:k1, (j % 4) * P:(j % 4 + 1) * P],
                                          ps[:, probs_bank(n), 0:(k1 - k0) * P].rearrange("p (k n) -> p k n", n=P)).then_inc(q["pte"], 1)

            def attended_low(h):
                dve.wait_ge(q["ath"], h + 1)
                r = slice(h * HALF, (h + 1) * HALF)
                nc.vector.tensor_tensor(at_lo[:, r], ps[:, AB[h], :], at_hi[:, r].bitcast(F32), ALU.subtract).then_inc(q["atl"], 1)

            def add_outputs(j):
                dve.wait_ge(q["exp"], j + 1)
                if first and j == 0:
                    dve.wait_ge(stored, 16 * TILES // STORE)
                chain.link(nc.vector.reciprocal(rinv[:, j:j + 1], rsum[:, j:j + 1]))
                nc.vector.tensor_scalar(w2[:, j, :], w[:, j, :], rinv[:, j:j + 1], None, ALU.mult).then_inc(q["w2"], 1)
                dve.wait_ge(q["w2"], j + 1)
                for n, e in enumerate((0, 1, 4, 5)):
                    z = 4 * j + e // 2
                    if n % 2 == 0:
                        dve.wait_ge(q["zz"], z + 1)
                    src = x if e == 0 else out
                    nc.vector.scalar_tensor_tensor(out[:, j, :], ps[:, OB[z], (e % 2) * C:(e % 2 + 1) * C], w2[:, j, e:e + 1],
                                                   src[:, j, :], ALU.mult, ALU.add).then_inc(q["z"], 1)
                    dve.wait_ge(q["z"], 4 * j + n + 1)

                if first and j >= 2:
                    statistics(j - 2)

            def other_outputs(j):
                add_scaled(nc.vector, dve, chain, j)

            def statistics(j):
                dve.wait_ge(*((q["res"], j + 1) if j < TILES - 1 else (q["last_res"], 1)))
                row_statistics(nc, m, chain, out, [j])

            work = {"s": row_max, "t": take_probs, "a": attended_low, "o": add_outputs, "O": other_outputs}
            route(0)
            for n in range(E + 2):
                masked(n)
                if n == 1:
                    route(1)
                if n == 3:
                    routing_weights()
            for e in range(E):
                run(work, early[e])
                if E + e + 2 < 2 * E:
                    masked(E + e + 2)
                elif e == E - 1 and not first:
                    dve.wait_ge(q["x"], 32)
                    row_statistics(nc, m, chain, m.xa, range(TILES))
            run(work, late + " O7")
            if first:
                statistics(TILES - 2)
                statistics(TILES - 1)

        @block.gpsimd
        def _(pool):
            chain = Chain(pool, q["pchain"])
            for j in range(TILES - 1):
                add_scaled(nc.gpsimd, pool, chain, j)

        @block.scalar
        def _(act):
            for n in range(4):
                h, ct = divmod(n, 2)
                act.wait_ge(q["tr"], n + 1)
                nc.scalar.copy(m.xt_hi[:, ct, h * HALF:(h + 1) * HALF], ps[:, XB[n], :]).then_inc(q["hi"], 1)
            for h in range(2):
                act.wait_ge(q["lt"], h + 1)
                nc.scalar.copy(lg_t[:, h * HALF:(h + 1) * HALF], ps[0:E, LT[h], :]).then_inc(q["ltc"], 1)
            act.wait_ge(q["m"], 2)
            nc.scalar.activation(w, gated, ACT.Exp).then_inc(q["gexp"], 1)
            def projected(h):
                r = slice(h * HALF, (h + 1) * HALF)
                act.wait_ge(q["qkv"], E * (h + 1))
                if h:
                    act.wait_ge(q["vt"], 1)
                nc.scalar.activation(qt[:, r], ps[:, QB[0], :], ACT.Copy, scale=float(D) ** -0.5).then_inc(q["ev"], 1)
                nc.scalar.copy(kt[:, r], ps[:, QB[1], :]).then_inc(q["ev"], 1)
                nc.scalar.copy(vt, ps[:, QB[2], :]).then_inc(q["ev"], 1)

            def take_values(h):
                act.wait_ge(q["vt"], h + 1)
                nc.scalar.copy(vv[:, 4 * h:4 * h + 4, :], ps[:, VB[h], :].rearrange("p (t d) -> p t d", t=4)).then_inc(q["v"], 1)

            def exponentials(i):
                act.wait_ge(q["nm"], i + 1)
                if i >= 2:
                    act.wait_ge(q["ptc"], before[i - 1])
                nc.scalar.activation(pp[:, i % 2, 0:(i + 1) * P], scores_of(i)[:, 0:(i + 1) * P], ACT.Exp, bias=nmax[:, i:i + 1],
                                     accum_out=rsum[:, i:i + 1]).then_inc(q["exp"], 1)

            def attended_high(h):
                act.wait_ge(q["pv"], h + 1)
                nc.scalar.copy(at_hi[:, h * HALF:(h + 1) * HALF], ps[:, AB[h], :]).then_inc(q["ath"], 1)

            def scale_outputs(j):
                act.wait_ge(q["w2"], j + 1)
                if j >= 2:
                    act.wait_ge(q["res"], j - 1)
                for e in (2, 3, 6, 7):
                    z = 4 * j + e // 2
                    if e % 2 == 0:
                        act.wait_ge(q["zz"], z + 1)
                    nc.scalar.activation(scaled[:, j % 2, e // 4 * 2 + e % 2, :], ps[:, OB[z], (e % 2) * C:(e % 2 + 1) * C], ACT.Copy,
                                         scale=w2[:, j, e:e + 1]).then_inc(q["y"], 1)

            work = {"v": take_values, "s": exponentials, "a": attended_high, "o": scale_outputs}
            projected(0)
            for e in range(E):
                run(work, early[e])
            projected(1)
            run(work, late.replace("s4 v1", "v1 s4"))

        @block.tensor
        def _(pe):
            for n in range(4):
                h, ct = divmod(n, 2)
                pe.wait_ge(q["xln"], 4 * h + 4)
                transpose_rows(nc, m, pe, m.xn, h, ct, XB[n]).then_inc(q["tr"], 1)
            for h in range(2):
                pe.wait_ge(q["lo"], 2 * h + 2)
                for ct in range(CT):
                    r = slice(h * HALF, (h + 1) * HALF)
                    last = three_pass(nc, ps[0:E, LT[h], :], m.sn_hi[:, ct], m.sn_lo[:, ct], m.xt_hi[:, ct, r], m.xt_lo[:, ct, r],
                                      ct == 0, ct == CT - 1)
                last.then_inc(q["lt"], 1)
            for h in range(2):
                pe.wait_ge(q["ltc"], h + 1)
                for t in range(4):
                    last = nc.tensor.transpose(ps[:, LG[h], t * E:(t + 1) * E], lg_t[:, h * HALF + t * P:h * HALF + (t + 1) * P],
                                               m.const[0:E, K_ID:K_ID + E])
                last.then_inc(q["lg"], 1)

            def mask_rows(n):
                h, e = divmod(n, E)
                if e == 0:
                    pe.wait_ge(q["m"], h + 1)
                if n >= 2:
                    pe.wait_ge(q["xm"], 2 * (n - 1))
                for t in range(4):
                    last = nc.tensor.matmul(ps[:, MB[n % 2], t * P:(t + 1) * P], m16[:, 4 * h + t, e:e + 1].to_broadcast([P, P]),
                                            m.ident16[:], start=True, stop=True)
                last.then_inc(q["mb"], 1)

            def project(n):
                h, e = divmod(n, E)
                pe.wait_ge(q["xm"], 2 * n + 2)
                if n == E:
                    pe.wait_ge(q["ev"], 3)
                for i in range(3):
                    for ct in range(CT):
                        last = three_pass(nc, ps[:, QB[i], :], m.w_hi[:, i, e * CT + ct], m.w_lo[:, i, e * CT + ct],
                                          xmh[:, n % XM, ct], xml[:, n % XM, ct], e == 0 and ct == 0, e == E - 1 and ct == CT - 1)
                last.then_inc(q["qkv"], 1)

            def values(h):
                pe.wait_ge(q["ev"], 3 * h + 3)
                for t in range(4):
                    last = nc.tensor.transpose(ps[:, VB[h], t * P:(t + 1) * P], vt[:, t * P:(t + 1) * P], m.const[:, K_ID:K_ID + P])
                last.then_inc(q["vt"], 1)

            def scores(i):
                pe.wait_ge(q["ev"], 6 if i >= 4 else 3)
                if i == 5:
                    pe.wait_ge(q["atl"], 1)
                if i >= 2:
                    pe.wait_ge(q["exp"], i - 1)
                n = (i + 1) * P
                for a in range(0, n, HALF):
                    z = min(n, a + HALF)
                    last = nc.tensor.matmul(ps[:, score_bank(i) + a // HALF, 0:z - a], qt[:, i * P:(i + 1) * P], kt[:, a:z],
                                            start=True, stop=True)
                last.then_inc(q["s"], 1)

            def turn_probs(j):
                pe.wait_ge(q["exp"], j + 1)
                if j == 0:
                    pe.wait_ge(q["v"], 1)
                for c, (k0, k1) in enumerate(chunks(j)):
                    n = before[j] + c
                    if n:
                        pe.wait_ge(q["pte"], n if n <= 4 else n - 1)
                    for k in range(k0, k1):
                        last = nc.tensor.transpose(ps[:, probs_bank(n), (k - k0) * P:(k - k0 + 1) * P],
                                                   pp[:, j % 2, k * P:(k + 1) * P], m.const[:, K_ID:K_ID + P])
                    last.then_inc(q["ptc"], 1)

            def attend(h):
                pe.wait_ge(q["pte"], before[4 * h + 4])
                pe.wait_ge(q["v"], h + 1)
                pe.wait_ge(q["exp"], 4 * h + 4)
                keys = 4 * h + 4
                for k in range(keys):
                    q0 = max(0, k - 4 * h) * P
                    last = nc.tensor.matmul(ps[:, AB[h], q0:HALF], vv[:, k, :], pt[h][:, k, q0:HALF], start=k == 0, stop=k == keys - 1)
                last.then_inc(q["pv"], 1)

            def outputs(j):
                pe.wait_ge(q["atl"], j // 4 + 1)
                if j == 0:
                    pe.wait_ge(q["v"], 2)
                for ep in range(4):
                    z = 4 * j + ep
                    if OB[z] in OB[:z]:
                        last_use = z - 1 - OB[:z][::-1].index(OB[z])
                        pe.wait_ge(q["z" if last_use % 2 == 0 else "y"], 2 * (last_use // 2 + 1))
                    r, c = slice(j * P, (j + 1) * P), slice(2 * ep * C, (2 * ep + 2) * C)
                    three_pass(nc, ps[:, OB[z], :], at_hi[:, r], at_lo[:, r], m.o_hi[:, c], m.o_lo[:, c], True, True).then_inc(q["zz"], 1)

            work = {"v": values, "s": scores, "t": turn_probs, "a": attend, "o": outputs}
            mask_rows(0)
            for n in range(2 * E):
                if n + 1 < 2 * E:
                    mask_rows(n + 1)
                project(n)
                if n >= E:
                    run(work, early[n - E])
            run(work, late)


ATT_SEMS = ("chain pchain u ss rs tr hi lo lat latc pj qkv sqd rsq rsp qn khi hl va xb qkt qkc s e "
            "at att an tr2 hi2 lo2 o r used")


def attention(nc, m, q, local):
    HS = H + KVH
    HP = TILES // 2
    v = m.carve(("qkv", TILES * QKV, F32), ("rot", TILES * QK, F32), ("t", HP * QK, F32), ("qe", HP * H * 4 * HD, F16),
                ("ke", HP * KVH * 8 * HD, F16), ("qt", TILES * S, F16), ("kt", KVH * S, F16), ("va", TILES * KVH * 32, F32),
                ("sums", HP * HS, F32), ("guess", HP * HS, F32), ("norms", HP * HS, F32), ("early", 2 * HP * QK, F32))
    U = m.xa
    qkv = v["qkv"].rearrange("p (t n) -> p t n", t=TILES)
    rot = v["rot"].rearrange("p (t n) -> p t n", t=TILES)
    qn = v["t"][:, 0:HP * H * HD].rearrange("p (n d) -> p n d", d=HD)
    kn = v["t"][:, HP * H * HD:].rearrange("p (n d) -> p n d", d=HD)
    qe = v["qe"].rearrange("p (n s d) -> p n s d", s=4, d=HD)
    ke = v["ke"].rearrange("p (n z s d) -> p n z s d", z=2, s=4, d=HD)
    qt = v["qt"].rearrange("p (r n) -> p r n", r=H // 2)
    kt = v["kt"].rearrange("p (g n) -> p g n", g=KVH)
    va = v["va"].rearrange("p (t g d) -> p t g d", t=TILES, g=KVH)
    place = [("early", 0), ("early", 1), ("qkv", 0), ("qkv", 1), ("qkv", 2), ("rot", 0)]
    pr = [v[name][:, i * 2 * HALF:(i + 1) * 2 * HALF].rearrange("p (j n) -> p j n", j=2) for name, i in place]
    rot_t = v["early"][:, 0:HP * QK]
    qt_word = TILES * QKV + TILES * QK + HP * QK + HP * H * 2 * HD + HP * KVH * 4 * HD
    squares = [v["early"][:, HP * QK:2 * HP * QK], m.at_xt_lo[:].rearrange("p t n -> p (t n)")[:, 0:HP * QK]]
    lat_t = m.at("lat", qt_word, S)[0:LAT, :]
    row_junk = m.at("junk", qt_word, TILES * C).rearrange("p (t c) -> p t c", t=TILES)
    at = [m.at_xt_lo[:, i, HALF:] for i in range(2)]
    ms, ss, rs, guess8 = (m.small[:, i, :] for i in (6, 2, 3, 4))
    rc = m.rc[:].rearrange("p (t h) -> p t h", t=4)
    ps, ps16 = m.ps, m.ps[:].bitcast(F16)
    cos = m.const[:, K_COS + 128 * local:K_COS + 128 * local + 64].rearrange("p (t f) -> p t f", t=TILES)
    sin = m.const[:, K_COS + 128 * local + 64:K_COS + 128 * local + 128].rearrange("p (t f) -> p t f", t=TILES)

    def rotary(h):
        r, shape = slice(HP * h, HP * h + HP), [P, HP, HS, HD // 2]
        pair = qkv[:, r, 0:QK].rearrange("p t (h f z) -> p t h f z", h=HS, z=2)
        to = rot[:, r, :].rearrange("p t (h f z) -> p t h f z", h=HS, z=2)
        cb, sb_ = (x[:, r, :].unsqueeze(2).to_broadcast(shape) for x in (cos, sin))
        return pair[:, :, :, :, 0], pair[:, :, :, :, 1], to, cb, sb_

    wo = GW + LW + (C if local else 0)
    XB, JB, LB = [0, 1, 6, 7], [2, 3], [4, 5]
    QKB = [6, 4, 5, 7, 0, 1] + 6 * [7]
    PIECES = [("k", 0), ("q", 0), ("q", 1), ("k", 2), ("q", 2), ("q", 3), ("k", 4), ("k", 6), ("q", 4), ("q", 5), ("q", 6), ("q", 7)]

    def piece(j):
        kind, t = PIECES[j]
        if kind == "q":
            return qt[:, :, t * P:(t + 1) * P], ps16[:, QKB[j], :].rearrange("p (r n) -> p r n", n=P)
        return (kt[:, :, t * P:(t + 2) * P].rearrange("p g (t n) -> p t g n", t=2),
                ps16[:, QKB[j], :].rearrange("p (t g n) -> p t g n", t=2, n=P))

    SB, VB, AB = [0, 2], [4, 5], 6
    OB = [7, 7, 0, 1]

    key_tiles, widths, unit_end, unit_tiles = [], [], [], []
    for h in range(2):
        for g in range(KVH):
            for k in range(4 * h + 4):
                a0, a1 = max(k * P, h * HALF), (h + 1) * HALF
                if local:
                    a1 = min(a1, k * P + SPAN)
                w = a1 - a0
                if w > 0:
                    key_tiles.append((g, h, k, a0, w, a0 - k * P, len(widths)))
                    widths += [2 * w] if 2 * w <= HALF else [w, w]
            unit_end.append(len(widths))
            unit_tiles.append(len(key_tiles))

    def places(i):
        w, n = key_tiles[i][4], key_tiles[i][6]
        return ((n, 0), (n, w)) if 2 * w <= HALF else ((n, 0), (n + 1, 0))

    plan, pending = [], []
    side = [("w", 1)] + [("q", j) for j in range(6, 12)]
    start = 3
    delay, pace = (3, 2) if local else (1, 1)
    for i in range(len(key_tiles) + LAG):
        if i == unit_tiles[3]:
            plan += side
            side = []
        s = [("s", 2 * i + a) for a in range(2)] if i < len(key_tiles) else []
        p = [("p", 2 * (i - LAG) + a) for a in range(2)] if i >= LAG else []
        cut = 1 if s and places(i)[0][0] != places(i)[1][0] else len(s)
        plan += s[:cut]
        due = [u for u in pending if i >= unit_tiles[u] + LAG - 1 + delay]
        plan += [("t", u) for u in due]
        if due == [KVH - 1]:
            side = [("x", 0), ("x", 1), ("o", 0), ("o", 1)]
        elif side and i >= start and (side[0][0] in "wq" or i % pace == 0):
            plan.append(side.pop(0))
        plan += p[:1] + s[cut:] + p[1:]
        pending = [u for u in pending if u not in due]
        if i >= LAG:
            ends = [u for u, end in enumerate(unit_tiles) if end == i - LAG + 1]
            plan += [("u", u) for u in ends]
            pending += ends
    plan += [("t", u) for u in pending] + side

    def follow(work):
        for kind, i in plan:
            if kind in work:
                work[kind](i)

    with nc.Block() as block:
        @block.gpsimd
        def _(pool):
            chain = Chain(pool, q["pchain"])
            chain.link(nc.gpsimd.memset(va, 0.0))
            chain.link(nc.gpsimd.memset(va[:, :, :, HD:HD + 1], 1.0))
            for h in range(2):
                r = slice(HP * h, HP * h + HP)
                pool.wait_ge(q["qkv"], HP * h + HP)
                even, odd, to, cb, sb_ = rotary(h)
                p1, p2 = (m.xn[:, i, :].rearrange("p t c -> p (t c)")[:, 0:HP * QK // 2].rearrange("p (t h f) -> p t h f", t=HP, h=HS)
                          for i in (slice(0, 4), slice(4, 8)))
                if h:
                    pool.wait_ge(q["rsp"], h)
                chain.done(nc.gpsimd.tensor_tensor(p1, even, sb_, ALU.mult))
                chain.link(nc.gpsimd.tensor_tensor(p2, odd, cb, ALU.mult))
                nc.gpsimd.tensor_tensor(to[:, :, :, :, 1], p1, p2, ALU.add).then_inc(q["rsp"], 1)
                nc.gpsimd.tensor_copy(va[:, r, :, 0:HD], qkv[:, r, QK:].rearrange("p t (g d) -> p t g d", d=HD)).then_inc(q["va"], 1)
            if local:
                for h in range(2):
                    r = slice(HP * h, HP * h + HP)
                    nc.gpsimd.tensor_tensor(m.xb[:, r, :], m.xb[:, r, :], U[:, r, :], ALU.add).then_inc(q["xb"], 1)

        @block.vector
        def _(dve):
            chain = Chain(dve, q["chain"])
            def row_scales():
                rsqrt(nc, chain, rs, guess8, ms)
                dve.sem_inc(q["rs"], 1)

            if not local:
                layernorm(nc, m, chain, m.xb, U, lambda ins: ins.then_inc(q["u"], 1))
                normed_mean_square(nc, m, chain, ms)
                chain.link(nc.vector.tensor_scalar(ms, ms, 1e-6, None, ALU.add))
                row_scales()
            for n in range(4):
                h, ct = divmod(n, 2)
                r = slice(h * HALF, (h + 1) * HALF)
                dve.wait_ge(q["hi"], n + 1)
                nc.vector.tensor_tensor(m.xt_lo[:, ct, r], ps[:, XB[n], :], m.xt_hi[:, ct, r].bitcast(F32),
                                        ALU.subtract).then_inc(q["lo"], 1)

            if local:
                dve.wait_ge(q["ss"], TILES)
                chain.link(nc.vector.tensor_scalar(ms, ss, 1.0 / C, 1e-6, ALU.mult, ALU.add))
                row_scales()

            def rope(h):
                even, odd, to, cb, sb_ = rotary(h)
                t1, t2 = (rot_t[:, i * HP * QK // 2:(i + 1) * HP * QK // 2].rearrange("p (t h f) -> p t h f", t=HP, h=HS) for i in range(2))
                dve.wait_ge(q["qkv"], HP * h + HP)
                if h:
                    dve.wait_ge(q["rsq"], h)
                chain.done(nc.vector.tensor_tensor(t1, even, cb, ALU.mult))
                chain.link(nc.vector.tensor_tensor(t2, odd, sb_, ALU.mult))
                nc.vector.tensor_tensor(to[:, :, :, :, 0], t1, t2, ALU.subtract).then_inc(q["rsq"], 1)

            sums, guess, norms = (v[n_] for n_ in ("sums", "guess", "norms"))

            def head_sums(h):
                dve.wait_ge(q["sqd"], h + 1)
                chain.link(nc.vector.tensor_reduce(sums, squares[h].rearrange("p (n d) -> p n d", d=HD), AX.X, ALU.add))

            def head_norms(h):
                chain.link(nc.vector.tensor_scalar(sums, sums, 1.0 / HD, 1e-6, ALU.mult, ALU.add))
                rsqrt(nc, chain, norms, guess, sums)
                dve.wait_ge(q["rsq"], h + 1)
                dve.wait_ge(q["rsp"], h + 1)
                nv = norms.rearrange("p (t h) -> p t h", t=HP)
                for o, h0, hn in ((kn, H, KVH), (qn, 0, H)):
                    nc.vector.tensor_tensor(o.rearrange("p (t h) d -> p t h d", t=HP),
                                            rot[:, HP * h:HP * h + HP, h0 * HD:(h0 + hn) * HD].rearrange("p t (h d) -> p t h d", d=HD),
                                            nv[:, :, h0:h0 + hn].unsqueeze(3).to_broadcast([P, HP, hn, HD]), ALU.mult).then_inc(q["qn"], 1)

            def two_parts(h):
                dve.wait_ge(q["qn"], 2 * (h + 1))
                if h:
                    dve.wait_ge(q["qkt"], 6)
                    for z in range(2):
                        chain.done(nc.vector.tensor_copy(ke[:, :, z, 0:2, :], kn.unsqueeze(2).to_broadcast([P, HP * KVH, 2, HD])))
                else:
                    dve.wait_ge(q["khi"], 2)
                chain.link(nc.vector.tensor_copy(qe[:, :, 0::2, :], qn.unsqueeze(2).to_broadcast([P, HP * H, 2, HD])))
                for z in range(2):
                    nc.vector.tensor_tensor(ke[:, :, z, 2:4, :], kn.unsqueeze(2).to_broadcast([P, HP * KVH, 2, HD]),
                                            ke[:, :, z, 0:2, :], ALU.subtract).then_inc(q["hl"], 1)
                nc.vector.tensor_tensor(qe[:, :, 1::2, :], qn.unsqueeze(2).to_broadcast([P, HP * H, 2, HD]), qe[:, :, 0::2, :],
                                        ALU.subtract).then_inc(q["hl"], 1)

            def take_piece(j):
                dve.wait_ge(q["qkt"], j + 1)
                to, src = piece(j)
                nc.vector.tensor_copy(to, src).then_inc(q["qkc"], 1)

            rope(0)
            head_sums(0)
            head_norms(0)
            two_parts(0)
            rope(1)
            take_piece(2)
            take_piece(5)
            head_sums(1)
            head_norms(1)

            def unit_out(u):
                dve.wait_ge(q["used"], unit_end[u])
                if u >= 2:
                    dve.wait_ge(q["att"], u - 1)
                nc.vector.tensor_copy(at[u % 2], ps[:, VB[u % 2], :]).then_inc(q["at"], 1)

            def unit_norm(u):
                h, g = divmod(u, KVH)
                dve.wait_ge(q["att"], u + 1)
                a = ps[:, AB, :].rearrange("p (t h d) -> p t h d", t=4, h=4)
                chain.link(nc.vector.reciprocal(rc, a[:, :, :, HD]))
                nc.vector.tensor_tensor(m.xn[:, 4 * h:4 * h + 4, g * 64:(g + 1) * 64].rearrange("p t (h d) -> p t h d", d=HD),
                                        a[:, :, :, 0:HD], rc.unsqueeze(3).to_broadcast([P, 4, 4, HD]), ALU.mult).then_inc(q["an"], 1)

            def take_rows(n):
                dve.wait_ge(q["tr2"], n + 1)
                r = slice(0, HALF)
                nc.vector.tensor_copy(m.xt_hi[:, n, r], ps[:, OB[0], :]).then_inc(q["hi2"], 1)
                dve.wait_ge(q["hi2"], n + 1)
                nc.vector.tensor_tensor(m.xt_lo[:, n, r], ps[:, OB[0], :], m.xt_hi[:, n, r].bitcast(F32), ALU.subtract).then_inc(q["lo2"], 1)

            def add_outputs(j):
                dve.wait_ge(q["o"], j + 1)
                both = slice(2 * j, 2 * j + 2)
                if local:
                    dve.wait_ge(q["xb"], j // 2 + 1)
                to = m.xb if local else U
                nc.vector.tensor_tensor(to[:, both, :], to[:, both, :], ps[:, OB[j], :].rearrange("p (t c) -> p t c", t=2),
                                        ALU.add).then_inc(q["r"], 1)

            def statistics(j):
                if local:
                    dve.wait_ge(q["r"], j + 1)
                    row_statistics(nc, m, chain, m.xb, (2 * j, 2 * j + 1))

            follow({"u": unit_out, "t": unit_norm, "w": two_parts, "q": take_piece, "x": take_rows, "o": add_outputs})
            for ct in range(2):
                dve.wait_ge(q["hi2"], ct + 3)
                nc.vector.tensor_tensor(m.xt_lo[:, ct, HALF:], ps[:, VB[ct], :], m.xt_hi[:, ct, HALF:].bitcast(F32),
                                        ALU.subtract).then_inc(q["lo2"], 1)
            statistics(0)
            statistics(1)
            for j in (2, 3):
                add_outputs(j)
                statistics(j)

        @block.scalar
        def _(act):
            def take_row_half(n):
                h, ct = divmod(n, 2)
                act.wait_ge(q["tr"], n + 1)
                nc.scalar.copy(m.xt_hi[:, ct, h * HALF:(h + 1) * HALF], ps[:, XB[n], :]).then_inc(q["hi"], 1)

            if local:
                for h in range(2):
                    for n in (2 * h, 2 * h + 1):
                        take_row_half(n)
                    for t in range(4 * h, 4 * h + 4):
                        nc.scalar.activation(row_junk[:, t, :], U[:, t, :], ACT.Square, accum_out=ss[:, t:t + 1]).then_inc(q["ss"], 1)
            else:
                for n in range(4):
                    take_row_half(n)
            act.wait_ge(q["rs"], 1)
            for h in range(2):
                if not local:
                    act.wait_ge(q["lat"], h + 1)
                    nc.scalar.copy(lat_t[:, h * HALF:(h + 1) * HALF], ps[0:LAT, LB[h], :]).then_inc(q["latc"], 1)
                for t in range(HP * h, HP * h + HP):
                    act.wait_ge(q["pj"], t + 1)
                    nc.scalar.activation(qkv[:, t, :], ps[:, JB[t % 2], 0:QKV], ACT.Copy, scale=rs[:, t:t + 1]).then_inc(q["qkv"], 1)
                act.wait_ge(q["qkv"], HP * h + HP)
                nc.scalar.activation(squares[h].rearrange("p (t n) -> p t n", t=HP), qkv[:, HP * h:HP * h + HP, 0:QK],
                                     ACT.Square).then_inc(q["sqd"], 1)
            act.wait_ge(q["qn"], 1)
            for z in range(2):
                nc.scalar.copy(ke[:, :, z, 0:2, :], kn.unsqueeze(2).to_broadcast([P, HP * KVH, 2, HD])).then_inc(q["khi"], 1)
            for j in (0, 1, 3, 4):
                act.wait_ge(q["qkt"], j + 1)
                to, src = piece(j)
                nc.scalar.copy(to, src).then_inc(q["qkc"], 1)
            act.wait_ge(q["va"], 2)
            act.wait_ge(q["rsq"], 2)

            def exponentials(pair):
                i, a = divmod(pair, 2)
                n = places(i)[a][0]
                if a == 0 and places(i)[1][0] == n:
                    return
                act.wait_ge(q["s"], n + 1)
                if n >= PR:
                    act.wait_ge(q["used"], n - PR + 1)
                nc.scalar.activation(pr[n % PR][:, :, 0:widths[n]], ps[:, SB[n % 2]:SB[n % 2] + 2, 0:widths[n]], ACT.Exp,
                                     scale=float(HD) ** -0.5).then_inc(q["e"], 1)

            follow({"s": exponentials})
            for ct in range(2):
                act.wait_ge(q["tr2"], ct + 3)
                nc.scalar.copy(m.xt_hi[:, ct, HALF:], ps[:, VB[ct], :]).then_inc(q["hi2"], 1)

        @block.tensor
        def _(pe):
            for n in range(4):
                h, ct = divmod(n, 2)
                if not local:
                    pe.wait_ge(q["u"], 4 * h + 4)
                transpose_rows(nc, m, pe, U, h, ct, XB[n]).then_inc(q["tr"], 1)
            for h in range(2):
                pe.wait_ge(q["lo"], 2 * h + 2)
                if not local:
                    r = slice(h * HALF, (h + 1) * HALF)
                    for ct in range(CT):
                        last = three_pass(nc, ps[:, LB[h], :], m.a_hi[:, ct, 0:P], m.a_lo[:, ct, 0:P], m.xt_hi[:, ct, r],
                                          m.xt_lo[:, ct, r], ct == 0, ct == CT - 1)
                    last.then_inc(q["lat"], 1)
                for t in range(4 * h, 4 * h + 4):
                    r = slice(t * P, (t + 1) * P)
                    if t >= 2:
                        pe.wait_ge(q["qkv"], t - 1)
                    c0, n = (GW, QKV) if local else (LAT, H * HD)
                    for ct in range(CT):
                        last = three_pass(nc, ps[:, JB[t % 2], 0:n], m.xt_hi[:, ct, r], m.xt_lo[:, ct, r],
                                          m.a_hi[:, ct, c0:c0 + n], m.a_lo[:, ct, c0:c0 + n], ct == 0, ct == CT - 1)
                    if not local:
                        pe.wait_ge(q["latc"], h + 1)
                        last = nc.tensor.matmul(ps[:, JB[t % 2], n:QKV], lat_t[:, r], m.kv_up[:], start=True, stop=True)
                    last.then_inc(q["pj"], 1)

            def turn_piece(j):
                kind, t = PIECES[j]
                pe.wait_ge(q["hl"], 3 * (t // HP) + (2 if kind == "k" else 3))
                if j >= 6:
                    pe.wait_ge(q["qkc"], j)
                if kind == "q":
                    for i in range(H // 2):
                        n = (t % HP) * H + 2 * i
                        src = qe[:, n:n + 2].rearrange("p h s d -> p (h s d)")
                        last = nc.tensor.transpose(ps16[:, QKB[j], i * P:(i + 1) * P], src, m.ident16[:])
                else:
                    for i in range(2 * KVH):
                        src = ke[:, (t % HP) * KVH + i].rearrange("p z s d -> p (z s d)")
                        last = nc.tensor.transpose(ps16[:, QKB[j], i * P:(i + 1) * P], src, m.ident16[:])
                last.then_inc(q["qkt"], 1)

            for j in range(6):
                turn_piece(j)
            pe.wait_ge(q["va"], 1)

            def scores(pair):
                i, a = divmod(pair, 2)
                g, h, k, q0, w, d, n0 = key_tiles[i]
                n, c0 = places(i)[a]
                if a == 0:
                    pe.wait_ge(q["qkc"], 6 * (h + 1))
                if n >= 2 and c0 == 0:
                    pe.wait_ge(q["e"], n - 1)
                keys = slice(k * P, (k + 1) * P)
                for j in range(2):
                    bank, rows = SB[n % 2] + j, slice(64 * j, 64 * j + 64)
                    if local:
                        if c0 == 0:
                            nc.tensor.matmul(ps[:, bank, 0:2 * w], m.ident16[:], m.win16[:, :, d:d + w], start=True, stop=False)
                        last = nc.tensor.matmul(ps[:, bank, c0:c0 + w], kt[rows, g, keys], qt[rows, 2 * g + a, q0:q0 + w],
                                                start=False, stop=a == 1)
                        continue
                    c = P if d == 0 else 0
                    if c:
                        nc.tensor.matmul(ps[:, bank, c0:c0 + c], m.ident16[:], m.tri16[:], start=True, stop=False)
                        last = nc.tensor.matmul(ps[:, bank, c0:c0 + c], kt[rows, g, keys], qt[rows, 2 * g + a, q0:q0 + c],
                                                start=False, stop=True)
                    if c < w:
                        last = nc.tensor.matmul(ps[:, bank, c0 + c:c0 + w], kt[rows, g, keys], qt[rows, 2 * g + a, q0 + c:q0 + w],
                                                start=True, stop=True)
                if a == 1 or places(i)[1][0] != n:
                    last.then_inc(q["s"], 1)

            def products(pair):
                i, a = divmod(pair, 2)
                g, h, k, q0, w, d, n0 = key_tiles[i]
                n, c0 = places(i)[a]
                u = h * KVH + g
                first = a == 0 and i == (unit_tiles[u - 1] if u else 0)
                if first and h and g == 0:
                    pe.wait_ge(q["va"], 2)
                if first and u >= 2:
                    pe.wait_ge(q["at"], u - 1)
                if first and local:
                    nc.tensor.matmul(ps[:, VB[u % 2], :], m.zeros16[:], m.zeros16[:].unsqueeze(1).to_broadcast([P, 4, P]),
                                     start=True, stop=True)
                pe.wait_ge(q["e"], n + 1)
                for j in range(2):
                    row = 32 * (2 * a + j)
                    o = ps[row:row + 32, VB[u % 2], q0 - h * HALF:q0 - h * HALF + w]
                    x = pr[n % PR][:, j, c0:c0 + w]
                    if local:
                        last = nc.tensor.matmul(o, va[:, k, g, :], x, start=False, stop=True, skip_group_check=True)
                    else:
                        last = nc.tensor.matmul(o, va[:, k, g, :], x, start=k == 0, stop=k == 4 * h + 3)
                if a == 1 or places(i)[1][0] != n:
                    last.then_inc(q["used"], 1)

            def turn(u):
                pe.wait_ge(q["at"], u + 1)
                if u:
                    pe.wait_ge(q["an"], u)
                for t in range(4):
                    last = nc.tensor.transpose(ps[:, AB, t * P:(t + 1) * P], at[u % 2][:, t * P:(t + 1) * P], m.const[:, K_ID:K_ID + P])
                last.then_inc(q["att"], 1)

            def turn_rows(ct):
                pe.wait_ge(q["an"], KVH)
                if ct:
                    pe.wait_ge(q["lo2"], ct)
                transpose_rows(nc, m, pe, m.xn, 0, ct, OB[0]).then_inc(q["tr2"], 1)

            def outputs(j):
                if j < 2:
                    pe.wait_ge(q["lo2"], 2)
                if j == 1:
                    pe.wait_ge(q["r"], 1)
                for t in (2 * j, 2 * j + 1):
                    r = slice(t * P, (t + 1) * P)
                    for ct in range(CT):
                        last = three_pass(nc, ps[:, OB[j], (t % 2) * C:(t % 2 + 1) * C], m.xt_hi[:, ct, r], m.xt_lo[:, ct, r],
                                          m.a_hi[:, ct, wo:wo + C], m.a_lo[:, ct, wo:wo + C], ct == 0, ct == CT - 1)
                last.then_inc(q["o"], 1)

            follow({"s": scores, "p": products, "t": turn, "q": turn_piece, "x": turn_rows, "o": outputs})
            pe.wait_ge(q["an"], 2 * KVH)
            for ct in range(2):
                transpose_rows(nc, m, pe, m.xn, 1, ct, VB[ct]).then_inc(q["tr2"], 1)
            pe.wait_ge(q["lo2"], 4)
            for j in (2, 3):
                outputs(j)


def build(nc, ins, out):
    ctx = ExitStack()
    with ctx:
        m = Mem(nc, ctx)
        qs = semaphores(nc, ctx, "setup", SETUP_SEMS)
        qa, qf = semaphores(nc, ctx, "att", ATT_SEMS), semaphores(nc, ctx, "ffn", FFN_SEMS)
        qo = semaphores(nc, ctx, "out", "stored")
        stored = qo["stored"]
        x = ins["L0_attn_hidden"]
        setup(nc, m, qs, stored, ins)
        with nc.Fori(0, B) as b:
            ffn(nc, m, qf, stored, b, x, out, True)
            clear(nc, dict(qf, **qo))
            for local in (False, True):
                attention(nc, m, qa, local)
                clear(nc, qa)
            ffn(nc, m, qf, stored, b, x, out, False)
            clear(nc, qf)
        with nc.Block() as block:
            @block.sync
            def _(sp):
                sp.wait_ge(stored, 16 * TILES // STORE)


_INS = ["L0_attn_hidden", "L0_attn_norm1_w", "L0_attn_norm2_w", "L0_attn_g_wq", "L0_attn_g_kv_down", "L0_attn_g_k_up",
        "L0_attn_g_v_up", "L0_attn_g_wo", "L0_attn_l_wq", "L0_attn_l_wk", "L0_attn_l_wv", "L0_attn_l_wo", "L0_ffn_sim_matrix",
        "L0_ffn_gates", "L0_ffn_q_proj", "L0_ffn_k_proj", "L0_ffn_v_proj", "L0_ffn_o_proj"]


def constants():
    import numpy as np
    c = np.zeros((P, K_ALL), np.float32)
    i, j = np.arange(P)[:, None], np.arange(P)[None, :]
    c[:, K_ID:K_ID + P] = i == j
    c[:, K_NEG:K_NEG + P] = np.where(j > i, -1e30, 0.0)
    c[:, K_TRI:K_TRI + P] = j >= i
    d = np.arange(SPAN)[None, :] - i
    c[:, K_WIN:K_WIN + SPAN] = (d >= 0) & (d < WIN)
    e = np.arange(E)
    c[:, K_TRI8:K_TRI8 + E * E] = (e[None, :] < e[:, None]).astype(np.float32).reshape(1, -1)
    for n, base in enumerate((1000000.0, 10000.0)):
        inv = (np.float32(1.0) / np.float32(base) ** (np.arange(0, HD, 2, dtype=np.float32) / np.float32(HD))).astype(np.float32)
        f = (np.arange(S, dtype=np.float32)[:, None] * inv[None, :]).reshape(TILES, P, HD // 2).transpose(1, 0, 2).reshape(P, 64)
        c[:, K_COS + 128 * n:K_COS + 128 * n + 64] = np.cos(f)
        c[:, K_COS + 128 * n + 64:K_COS + 128 * n + 128] = np.sin(f)
    return c


def kernel(**inputs):
    import numpy as np
    import concourse.bacc as bacc
    from concourse.bass_utils import run_bass_kernel_spmd

    nc = bacc.Bacc("TRN2", target_bir_lowering=False, num_devices=1)
    arrays, ins = {}, {}
    for name in _INS:
        a = np.ascontiguousarray(inputs[name])
        arrays[f"in_{name}"] = a
        ins[name] = nc.dram_tensor(f"in_{name}", a.shape, mybir.dt.from_np(a.dtype), kind="ExternalInput").ap()
    arrays["in_const"] = constants()
    ins["const"] = nc.dram_tensor("in_const", (P, K_ALL), F32, kind="ExternalInput").ap()
    out = nc.dram_tensor("out_dram", (B, S, C), F32, kind="ExternalOutput").ap()
    build(nc, ins, out)
    r = run_bass_kernel_spmd(nc, [arrays], core_ids=[0])
    return r.results[0]["out_dram"]
```
